# Optimizing a Trainium2 kernel written in Bass

```python
import numpy as np
import jax
import jax.numpy as jnp

def _softmax(x, axis=-1):
    return jax.nn.softmax(x, axis=axis)

def _gelu(x):
    return jax.nn.gelu(x, approximate=True)

def _silu(x):
    return jax.nn.silu(x)

def _sigmoid(x):
    return jax.nn.sigmoid(x)

def _layernorm(x, axis=-1, eps=1e-05):
    m = jnp.mean(x, axis=axis, keepdims=True)
    v = jnp.var(x, axis=axis, keepdims=True)
    return (x - m) / jnp.sqrt(v + eps)

def _scatter_add(tgt, idx, src, axis=0):
    return tgt.at[idx].add(src)

def _segment_sum(src, seg, n):
    return jax.ops.segment_sum(src, seg, n)
kernel_name = 'mk_rec_standalone_d1_rec_r8_c638b6'

def setup_inputs(seed: int=0):
    np.random.seed(seed)
    _w = jnp.asarray

    def _rec_inputs():
        import jax
        import jax.numpy as jnp
        _rk = jax.random.key(seed)
        r_idx = jnp.stack([jax.random.randint(jax.random.fold_in(jax.random.fold_in(_rk, 1), 0), (2048,), 0, 99999, jnp.int32), jax.random.randint(jax.random.fold_in(jax.random.fold_in(_rk, 1), 1), (2048,), 0, 12499, jnp.int32), jax.random.randint(jax.random.fold_in(jax.random.fold_in(_rk, 1), 2), (2048,), 4, 99997, jnp.int32), jax.random.randint(jax.random.fold_in(jax.random.fold_in(_rk, 1), 3), (2048,), 2, 99997, jnp.int32), jax.random.randint(jax.random.fold_in(jax.random.fold_in(_rk, 1), 4), (2048,), 1, 99988, jnp.int32), jax.random.randint(jax.random.fold_in(jax.random.fold_in(_rk, 1), 5), (2048,), 1, 99996, jnp.int32), jax.random.randint(jax.random.fold_in(jax.random.fold_in(_rk, 1), 6), (2048,), 12, 99997, jnp.int32), jax.random.randint(jax.random.fold_in(jax.random.fold_in(_rk, 1), 7), (2048,), 17, 99995, jnp.int32), jax.random.randint(jax.random.fold_in(jax.random.fold_in(_rk, 1), 8), (2048,), 0, 99998, jnp.int32), jax.random.randint(jax.random.fold_in(jax.random.fold_in(_rk, 1), 9), (2048,), 0, 99998, jnp.int32), jax.random.randint(jax.random.fold_in(jax.random.fold_in(_rk, 1), 10), (2048,), 3, 99993, jnp.int32), jax.random.randint(jax.random.fold_in(jax.random.fold_in(_rk, 1), 11), (2048,), 0, 99993, jnp.int32), jax.random.randint(jax.random.fold_in(jax.random.fold_in(_rk, 1), 12), (2048,), 1, 99988, jnp.int32), jax.random.randint(jax.random.fold_in(jax.random.fold_in(_rk, 1), 13), (2048,), 0, 99997, jnp.int32), jax.random.randint(jax.random.fold_in(jax.random.fold_in(_rk, 1), 14), (2048,), 3, 99993, jnp.int32), jax.random.randint(jax.random.fold_in(jax.random.fold_in(_rk, 1), 15), (2048,), 10, 99994, jnp.int32), jax.random.randint(jax.random.fold_in(jax.random.fold_in(_rk, 1), 16), (2048,), 10, 99998, jnp.int32), jax.random.randint(jax.random.fold_in(jax.random.fold_in(_rk, 1), 17), (2048,), 18, 99979, jnp.int32), jax.random.randint(jax.random.fold_in(jax.random.fold_in(_rk, 1), 18), (2048,), 1, 99996, jnp.int32), jax.random.randint(jax.random.fold_in(jax.random.fold_in(_rk, 1), 19), (2048,), 6, 99987, jnp.int32), jax.random.randint(jax.random.fold_in(jax.random.fold_in(_rk, 1), 20), (2048,), 6, 12500, jnp.int32), jax.random.randint(jax.random.fold_in(jax.random.fold_in(_rk, 1), 21), (2048,), 2, 12500, jnp.int32), jax.random.randint(jax.random.fold_in(jax.random.fold_in(_rk, 1), 22), (2048,), 7, 12498, jnp.int32), jax.random.randint(jax.random.fold_in(jax.random.fold_in(_rk, 1), 23), (2048,), 2, 99999, jnp.int32), jax.random.randint(jax.random.fold_in(jax.random.fold_in(_rk, 1), 24), (2048,), 29, 99990, jnp.int32), jax.random.randint(jax.random.fold_in(jax.random.fold_in(_rk, 1), 25), (2048,), 10, 99986, jnp.int32)], axis=1)
        return r_idx
    r_idx = _rec_inputs()

    def _L0_rec_setup():
        import jax, jax.numpy as jnp
        import numpy as np
        B, F, V, E = (2048, 26, 12500, 16)
        D1, D2 = (64, 32)
        key = jax.random.key(seed)
        ks = jax.random.split(key, 10)
        s = 0.01
        return dict(idx=jax.random.randint(ks[0], (B, F), 0, V, dtype=jnp.int32), fm_emb=jax.random.normal(ks[1], (F, V, E), jnp.float32) * s, dnn_emb=jax.random.normal(ks[2], (F, V, E), jnp.float32) * s, lin_w=jax.random.normal(ks[3], (F, V), jnp.float32) * s, fm_bias=jnp.zeros((), jnp.float32), W1=jax.random.normal(ks[4], (F * E, D1), jnp.float32) / np.sqrt(F * E), b1=jnp.zeros((D1,), jnp.float32), W2=jax.random.normal(ks[5], (D1, D2), jnp.float32) / np.sqrt(D1), b2=jnp.zeros((D2,), jnp.float32), W3=jax.random.normal(ks[6], (D2, 1), jnp.float32) / np.sqrt(D2), b3=jnp.zeros((1,), jnp.float32), Wf=jax.random.normal(ks[7], (2, 1), jnp.float32) / np.sqrt(2.0), bf=jnp.zeros((1,), jnp.float32))
    _L0_rec_all = _L0_rec_setup()
    _L0_rec_in = {k: v for k, v in _L0_rec_all.items() if k in ('fm_emb', 'dnn_emb', 'lin_w', 'fm_bias', 'W1', 'b1', 'W2', 'b2', 'W3', 'b3', 'Wf', 'bf')}
    del _L0_rec_all
    return {'r_idx': r_idx, 'L0_rec_fm_emb': _L0_rec_in['fm_emb'], 'L0_rec_dnn_emb': _L0_rec_in['dnn_emb'], 'L0_rec_lin_w': _L0_rec_in['lin_w'], 'L0_rec_fm_bias': _L0_rec_in['fm_bias'], 'L0_rec_W1': _L0_rec_in['W1'], 'L0_rec_b1': _L0_rec_in['b1'], 'L0_rec_W2': _L0_rec_in['W2'], 'L0_rec_b2': _L0_rec_in['b2'], 'L0_rec_W3': _L0_rec_in['W3'], 'L0_rec_b3': _L0_rec_in['b3'], 'L0_rec_Wf': _L0_rec_in['Wf'], 'L0_rec_bf': _L0_rec_in['bf']}

def reference(r_idx, L0_rec_fm_emb, L0_rec_dnn_emb, L0_rec_lin_w, L0_rec_fm_bias, L0_rec_W1, L0_rec_b1, L0_rec_W2, L0_rec_b2, L0_rec_W3, L0_rec_b3, L0_rec_Wf, L0_rec_bf):
    import jax
    import jax.numpy as jnp

    def _L0_rec_ref(idx, fm_emb, dnn_emb, lin_w, fm_bias, W1, b1, W2, b2, W3, b3, Wf, bf):
        import jax, jax.numpy as jnp
        import numpy as np
        B, F, V, E = (2048, 26, 12500, 16)
        D1, D2 = (64, 32)
        f_ix = jnp.arange(F)[None, :]
        linear_term = fm_bias + lin_w[f_ix, idx].sum(axis=1)
        e = fm_emb[f_ix, idx]
        s = e.sum(axis=1)
        sum_of_square = (s * s).sum(axis=-1)
        square_of_sum = (e * e).sum(axis=(1, 2))
        fm_out = linear_term + 0.5 * (sum_of_square - square_of_sum)
        d = dnn_emb[f_ix, idx].reshape(B, F * E)
        h = jax.nn.relu(d @ W1 + b1)
        h = jax.nn.relu(h @ W2 + b2)
        dnn_out = (h @ W3 + b3)[:, 0]
        comb = jnp.stack([fm_out, dnn_out], axis=1)
        return jax.nn.sigmoid((comb @ Wf + bf)[:, 0])
    y = _L0_rec_ref(r_idx, L0_rec_fm_emb, L0_rec_dnn_emb, L0_rec_lin_w, L0_rec_fm_bias, L0_rec_W1, L0_rec_b1, L0_rec_W2, L0_rec_b2, L0_rec_W3, L0_rec_b3, L0_rec_Wf, L0_rec_bf)
    return y

_drawn_inputs = setup_inputs


def setup_inputs(seed=0):
    import zlib

    import numpy as np

    out = dict(_drawn_inputs(seed))
    spreads = {'L0_rec_b1': (0.0, 0.355), 'L0_rec_b2': (0.0, 0.1)}
    factors = {'L0_rec_fm_emb': 30.897,
     'L0_rec_dnn_emb': 8.0,
     'L0_rec_lin_w': 64.0,
     'L0_rec_W1': 8.0,
     'L0_rec_W2': 3.416}
    for name, (base, spread) in spreads.items():
        noise = np.random.default_rng([zlib.crc32(name.encode()), seed]).standard_normal(out[name].shape)
        drawn = base * np.exp(spread * noise) if base else spread * noise
        out[name] = jnp.asarray(drawn.astype(out[name].dtype))
    for name, factor in factors.items():
        out[name] = (out[name] * factor).astype(out[name].dtype)
    return out
```

```python
from contextlib import ExitStack

import concourse.bass as bass
from concourse import mybir

P = 128
F32 = mybir.dt.float32
I32 = mybir.dt.int32
U32 = mybir.dt.uint32
ALU = mybir.AluOpType
ACT = mybir.ActivationFunctionType
AX = mybir.AxisListType


def deepfm_kernel(nc, r_idx, rows_dram, fm_bias, W1, b1, W2, b2, W3, b3, Wf, bf, out, V):
    B, F = r_idx.shape
    ROW = rows_dram.shape[1]
    D1, D2 = W2.shape
    E = W1.shape[0] // F
    TILES = B // P
    DNN, FM, LIN = slice(0, E), slice(E, 2 * E), 2 * E
    assert ROW == 2 * E + 1 and TILES % 2 == 0

    HEAD, STEP = 8, 2
    TAIL = F - HEAD
    ROUNDS = -(-F // 8)
    LIST = 8 * ROUNDS
    PER = P // E
    CHUNKS = [(f, min(PER, F - f)) for f in range(0, F, PER)]
    FULL = F // PER
    REST = (F - FULL * PER) * E
    assert len(CHUNKS) == FULL + 1

    with ExitStack() as ctx:
        def sb(name, shape, dt=F32):
            return ctx.enter_context(nc.sbuf_tensor(name, shape, dt))

        def bank(name, dt=F32):
            return ctx.enter_context(nc.psum_tensor(name, [P, 512], dt))

        def sem(name):
            return ctx.enter_context(nc.semaphore(name))

        field_base = sb("field_base", [P, F])
        ident = sb("ident", [P, P])
        last_rows = sb("last_rows", [P, F, ROW])
        w1 = sb("w1", [P, len(CHUNKS), D1])
        w2 = sb("w2", [D1, D2])
        w3 = sb("w3", [D2, 1])
        b1c = sb("b1c", [D1, 1])
        b2c = sb("b2c", [D2, 1])
        scal = sb("scal", [P, 5])
        fm_bias_c, b3_c, bf_c, wf0_c, wf1_c = (scal[:, i:i + 1] for i in range(5))
        const_c = sb("const_c", [P, 2])

        idx = sb("idx", [P, TILES, F], I32)
        capped = sb("capped", [P, TILES, F])
        wrap = sb("wrap", [P, TILES, F])
        value = sb("value", [P, TILES, F])
        listed = sb("listed", [P, TILES, F])
        key1 = sb("key1", [P, TILES, F])
        keys = sb("keys", [P, TILES + 1, F])
        length = sb("length", [P, TILES])
        longest = sb("longest", [TILES, 1])
        longest_row = sb("longest_row", [1, TILES])
        longest_i = sb("longest_i", [1, TILES], I32)
        assert TAIL % STEP == 0
        STEPS = TAIL // STEP
        step_start = sb("step_start", [1, STEPS])
        step_taken = sb("step_taken", [1, TILES, STEPS])
        steps_taken = sb("steps_taken", [1, TILES])
        steps_so_far = sb("steps_so_far", [1, TILES])
        no_steps = sb("no_steps", [1, TILES])
        tail_count = sb("tail_count", [1, TILES + 1], I32)
        work = [sb(f"work{i}", [P, F]) for i in range(2)]
        tile_keys = [sb(f"tile_keys{i}", [P, F]) for i in range(2)]
        top = sb("top", [P, LIST])
        entry_key = sb("entry_key", [P, LIST])
        entry_row = [sb(f"entry_row{i}", [P, LIST], U32) for i in range(2)]

        packed = [sb(f"packed{i}", [P, F, ROW]) for i in range(2)]
        placed = [sb(f"placed{i}", [P, F, ROW]) for i in range(2)]
        dnn_in = [sb(f"dnn_in{i}", [P, F * E]) for i in range(2)]
        square_sink = sb("square_sink", [P, F, E])
        dnn_t = [sb(f"dnn_t{i}", [P, len(CHUNKS), P]) for i in range(2)]
        h1 = sb("h1", [D1, P])
        h2 = sb("h2", [D2, P])

        fm_sum = sb("fm_sum", [P, TILES, E])
        fm_sum_sq = sb("fm_sum_sq", [P, TILES, E])
        sq_of_sum = sb("sq_of_sum", [P, TILES])
        sum_of_sq = sb("sum_of_sq", [P, TILES])
        linear = sb("linear", [P, TILES])
        pair_diff = sb("pair_diff", [P, TILES])
        fm_out = sb("fm_out", [P, TILES])
        dnn_part = sb("dnn_part", [P, TILES])
        logit = sb("logit", [P, TILES])
        y = sb("y", [P, TILES])

        HALF = F // 2
        match = [[bank(f"match{i}{h}", I32)[:, 0:HALF * F].rearrange("p (j f) -> p j f", f=F) for h in range(2)]
                 for i in range(2)]
        dnn_tp = [bank(f"dnn_tp{i}")[:].rearrange("p (c b) -> p c b", b=P) for i in range(2)]
        hidden_ps = bank("hidden_ps")
        h1_ps, h2_ps = hidden_ps[0:D1, 0:P], hidden_ps[0:D2, P:2 * P]
        ends_ps = bank("ends_ps")
        len_ps, dnn_ps = ends_ps[:, 0:P], ends_ps[:, P:P + TILES]

        waits_over = sem("waits_over")
        idx_loaded = sem("idx_loaded")
        last_loaded = sem("last_loaded")
        w1_loaded = sem("w1_loaded")
        small_loaded = sem("small_loaded")
        base_made = sem("base_made")
        ident_made = sem("ident_made")
        key_step = sem("key_step")
        lengths_made = sem("lengths_made")
        lengths_t = sem("lengths_t")
        longest_made = sem("longest_made")
        longest_t = sem("longest_t")
        longest_known = sem("longest_known")
        list_step = sem("list_step")
        list_made = sem("list_made")
        head_landed = sem("head_landed")
        tail_landed = sem("tail_landed")
        entry_placed = sem("entry_placed")
        match_made = sem("match_made")
        defaults_set = sem("defaults_set")
        tile_placed = sem("tile_placed")
        fm_summed = sem("fm_summed")
        squared = sem("squared")
        dnn_in_made = sem("dnn_in_made")
        transposed = sem("transposed")
        dnn_t_kept = sem("dnn_t_kept")
        h1_done = sem("h1_done")
        h1_kept = sem("h1_kept")
        h2_done = sem("h2_done")
        h2_kept = sem("h2_kept")
        dnn_done = sem("dnn_done")
        const_step = sem("const_step")
        end_step = sem("end_step")
        logit_done = sem("logit_done")
        y_done = sem("y_done")
        stored = sem("stored")

        def wait_alone(eng, semaphore, count):
            eng.wait_ge(semaphore, count)
            eng.sem_inc(waits_over, 1)

        block = ctx.enter_context(nc.Block())

        @block.sync
        def _(sp):
            sp.dma_start(idx[:], r_idx.rearrange("(p t) f -> p t f", p=P)).then_inc(idx_loaded, 16)
            last = rows_dram.rearrange("(f v) r -> f v r", v=V)[:, V - 1, :]
            sp.dma_start(last_rows[:], last.unsqueeze(0).broadcast_to([P, F, ROW])).then_inc(last_loaded, 16)
            sp.dma_start(w1[:, 0:FULL, :], W1[0:FULL * P, :].rearrange("(c k) n -> k c n", k=P)
                         ).then_inc(w1_loaded, 16)
            sp.dma_start(w1[0:REST, FULL, :], W1[FULL * P:FULL * P + REST, :]).then_inc(w1_loaded, 16)
            sp.wait_ge(y_done, 1)
            sp.dma_start(out.rearrange("(p t) -> p t", p=P), y[:]).then_inc(stored, 16)
            sp.wait_ge(stored, 16)

        @block.gpsimd
        def _(pool):
            nc.gpsimd.iota(step_start[:], [[STEP, STEPS]], base=HEAD, channel_multiplier=0,
                           allow_small_or_imprecise_dtypes=True)
            nc.gpsimd.iota(field_base[:], [[V, F]], base=1, channel_multiplier=0,
                           allow_small_or_imprecise_dtypes=True).then_inc(base_made, 1)
            nc.gpsimd.memset(ident[:], 0.0).then_inc(ident_made, 1)
            pool.wait_ge(ident_made, 1)
            nc.gpsimd.affine_select(out=ident[:], in_=ident[:], compare_op=ALU.not_equal, fill=1.0, base=0,
                                    pattern=[[-1, P]], channel_multiplier=1).then_inc(ident_made, 1)

            def fetch(k, j, landed):
                nc.gpsimd.indirect_dma_start(
                    out=packed[k][:, j, :], out_offset=None, in_=rows_dram,
                    in_offset=bass.IndirectOffsetOnAxis(ap=entry_row[k][:, j:j + 1], axis=0),
                ).then_inc(landed, 16)

            def fetch_tail(k, j, n):
                with pool.If(n > j):
                    for i in range(j, min(j + STEP, F)):
                        fetch(k, i, tail_landed)
                    if j + STEP < F:
                        fetch_tail(k, j + STEP, n)

            with pool.Fori(0, TILES // 2) as pair:
                for k in range(2):
                    t = 2 * pair + k
                    pool.wait_ge(head_landed, 16 * HEAD * t)
                    wait_alone(pool, list_made, t + 1)
                    for j in range(HEAD):
                        fetch(k, j, head_landed)
                    pool.wait_ge(longest_known, 2)
                    n = pool.value_load(longest_i[0:1, bass.ds(t, 1)], min_val=0, max_val=F)
                    before = pool.value_load(tail_count[0:1, bass.ds(t, 1)], min_val=0, max_val=16 * TAIL * TILES)
                    wait_alone(pool, tail_landed, before)
                    fetch_tail(k, HEAD, n)

        @block.vector
        def _(dve):
            steps = [0]

            def key_made(ins):
                ins.then_inc(key_step, 1)
                steps[0] += 1
                dve.wait_ge(key_step, steps[0])

            nc.vector.memset(keys[:, TILES, :], 0.0)
            dve.wait_ge(idx_loaded, 16)
            key_made(nc.vector.tensor_scalar(capped[:], idx[:], float(V - 1), float(-V), ALU.min, ALU.max))
            key_made(nc.vector.tensor_scalar(wrap[:], capped[:], 0.0, float(V), ALU.is_lt, ALU.mult))
            key_made(nc.vector.tensor_tensor(value[:], capped[:], wrap[:], ALU.add))
            nc.vector.tensor_scalar(listed[:], value[:], float(V - 1), None, ALU.is_lt)
            dve.wait_ge(base_made, 1)
            key_made(nc.vector.tensor_tensor(key1[:], value[:],
                                             field_base[:].unsqueeze(1).broadcast_to([P, TILES, F]), ALU.add))
            key_made(nc.vector.tensor_tensor(keys[:, 0:TILES, :], key1[:], listed[:], ALU.mult))

            def make_list(k, t):
                dve.sem_clear(list_step)
                done = [0]

                def made(ins):
                    ins.then_inc(list_step, 1)
                    done[0] += 1
                    dve.wait_ge(list_step, done[0])

                made(nc.vector.tensor_copy(tile_keys[k][:], keys[:, bass.ds(t, 1), :].rearrange("p o f -> p (o f)")))
                src = tile_keys[k]
                for r in range(ROUNDS):
                    eight = top[:, 8 * r:8 * r + 8]
                    made(nc.vector.max(eight, src[:]))
                    if r + 1 < ROUNDS:
                        made(nc.vector.match_replace(work[r % 2][:], eight, src[:], 0.0))
                        src = work[r % 2]
                made(nc.vector.tensor_scalar(entry_key[:], top[:], 1.0, None, ALU.max))
                nc.vector.tensor_scalar(entry_row[k][:], entry_key[:], -1.0, None, ALU.add).then_inc(list_made, 1)
                for h in range(2):
                    nc.vector.tensor_tensor(match[k][h],
                                            tile_keys[k][:].unsqueeze(1).broadcast_to([P, HALF, F]),
                                            entry_key[:, h * HALF:(h + 1) * HALF].unsqueeze(2)
                                            .broadcast_to([P, HALF, F]),
                                            ALU.is_equal).then_inc(match_made, 1)

            def place(k, j):
                m = F - j
                if j:
                    dve.wait_ge(entry_placed, j)
                nc.vector.copy_predicated(
                    placed[k][:, 0:m, :],
                    match[k][j // HALF][:, j % HALF, 0:m].unsqueeze(2).broadcast_to([P, m, ROW]),
                    packed[k][:, j, :].unsqueeze(1).broadcast_to([P, m, ROW])).then_inc(entry_placed, 1)

            def place_tail(k, j, n):
                with dve.If(n > j):
                    for i in range(j, min(j + STEP, F)):
                        place(k, i)
                    if j + STEP < F:
                        place_tail(k, j + STEP, n)
                    else:
                        dve.wait_ge(entry_placed, F)
                with dve.Else():
                    dve.wait_ge(entry_placed, j)

            make_list(0, 0)
            nc.vector.tensor_reduce(length[:], listed[:], AX.X, ALU.add).then_inc(lengths_made, 1)
            dve.wait_ge(lengths_t, 1)
            nc.vector.tensor_reduce(longest[:], len_ps[0:TILES, :], AX.X, ALU.max).then_inc(longest_made, 1)
            dve.wait_ge(longest_t, 1)
            nc.vector.tensor_copy(longest_i[:], len_ps[0:1, 0:TILES]).then_inc(longest_known, 1)
            nc.vector.memset(no_steps[:], 0.0)
            nc.vector.memset(tail_count[:], 0)
            key_made(nc.vector.tensor_copy(longest_row[:], len_ps[0:1, 0:TILES]))
            key_made(nc.vector.tensor_tensor(step_taken[:],
                                             longest_row[:].unsqueeze(2).broadcast_to([1, TILES, STEPS]),
                                             step_start[:].unsqueeze(1).broadcast_to([1, TILES, STEPS]), ALU.is_gt))
            key_made(nc.vector.tensor_reduce(steps_taken[:], step_taken[:], AX.X, ALU.add))
            key_made(nc.vector.tensor_tensor_scan(steps_so_far[:], steps_taken[:], no_steps[:], 0.0, ALU.add, ALU.add))
            nc.vector.tensor_scalar(tail_count[:, 1:TILES + 1], steps_so_far[:], 16.0 * STEP, None, ALU.mult
                                    ).then_inc(longest_known, 1)

            dve.wait_ge(small_loaded, 16 * 8)
            nc.vector.tensor_scalar(const_c[:, 0:1], b3_c, wf1_c, bf_c, ALU.mult, ALU.add).then_inc(const_step, 1)
            dve.wait_ge(const_step, 1)
            nc.vector.tensor_scalar(const_c[:, 1:2], fm_bias_c, wf0_c, const_c[:, 0:1], ALU.mult, ALU.add
                                    ).then_inc(const_step, 1)
            dve.wait_ge(longest_known, 2)

            with dve.Fori(0, TILES // 2) as pair:
                for k in range(2):
                    t = 2 * pair + k
                    make_list(1 - k, t + 1)
                    n = dve.value_load(longest_i[0:1, bass.ds(t, 1)], min_val=0, max_val=F)
                    after = dve.value_load(tail_count[0:1, bass.ds(t + 1, 1)], min_val=0, max_val=16 * TAIL * TILES)
                    wait_alone(dve, match_made, 2 * (t + 1))
                    wait_alone(dve, defaults_set, t + 1)
                    wait_alone(dve, head_landed, 16 * HEAD * (t + 1))
                    dve.sem_clear(entry_placed)
                    for j in range(HEAD):
                        place(k, j)
                    wait_alone(dve, tail_landed, after)
                    place_tail(k, HEAD, n)
                    nc.vector.tensor_reduce(fm_sum[:, bass.ds(t, 1), :],
                                            placed[k][:, :, FM].rearrange("p f e -> p e f").unsqueeze(1),
                                            AX.X, ALU.add).then_inc(fm_summed, 1)
                    nc.vector.tensor_reduce(linear[:, bass.ds(t, 1)], placed[k][:, :, LIN],
                                            AX.X, ALU.add).then_inc(fm_summed, 1)

            def ended(n, ins):
                ins.then_inc(end_step, 1)
                dve.wait_ge(end_step, n)

            dve.wait_ge(fm_summed, 2 * TILES)
            ended(1, nc.vector.tensor_tensor(fm_sum_sq[:], fm_sum[:], fm_sum[:], ALU.mult))
            ended(2, nc.vector.tensor_reduce(sq_of_sum[:], fm_sum_sq[:], AX.X, ALU.add))
            dve.wait_ge(squared, TILES)
            ended(3, nc.vector.tensor_tensor(pair_diff[:], sq_of_sum[:], sum_of_sq[:], ALU.subtract))
            ended(4, nc.vector.scalar_tensor_tensor(out=fm_out[:], in0=pair_diff[:], scalar=0.5, in1=linear[:],
                                                    op0=ALU.mult, op1=ALU.add))
            dve.wait_ge(const_step, 2)
            dve.wait_ge(dnn_done, TILES)
            ended(5, nc.vector.tensor_scalar(dnn_part[:], dnn_ps, wf1_c, const_c[:, 1:2], ALU.mult, ALU.add))
            nc.vector.scalar_tensor_tensor(out=logit[:], in0=fm_out[:], scalar=wf0_c, in1=dnn_part[:],
                                           op0=ALU.mult, op1=ALU.add).then_inc(logit_done, 1)

        @block.tensor
        def _(pe):
            pe.wait_ge(ident_made, 2)
            pe.wait_ge(lengths_made, 1)
            nc.tensor.transpose(len_ps[0:TILES, :], length[:], ident[:]).then_inc(lengths_t, 1)
            pe.wait_ge(longest_made, 1)
            nc.tensor.transpose(len_ps[0:1, 0:TILES], longest[:], ident[0:TILES, 0:TILES]).then_inc(longest_t, 1)
            pe.wait_ge(w1_loaded, 32)
            pe.wait_ge(small_loaded, 16 * 8)

            with pe.Fori(0, TILES // 2) as pair:
                for k in range(2):
                    t = 2 * pair + k
                    pe.wait_ge(dnn_in_made, t + 1)
                    for c, (f, n) in enumerate(CHUNKS):
                        last = nc.tensor.transpose(dnn_tp[k][0:n * E, c, :], dnn_in[k][:, f * E:(f + n) * E], ident[:])
                    last.then_inc(transposed, 1)
                    pe.wait_ge(dnn_t_kept, 2 * (t + 1))
                    for c, (f, n) in enumerate(CHUNKS):
                        last = nc.tensor.matmul(h1_ps, lhsT=w1[0:n * E, c, :], rhs=dnn_t[k][0:n * E, c, :],
                                                start=c == 0, stop=c == FULL)
                    last.then_inc(h1_done, 1)
                    wait_alone(pe, h1_kept, t + 1)
                    nc.tensor.matmul(h2_ps, lhsT=w2[:], rhs=h1[:], start=True, stop=True).then_inc(h2_done, 1)
                    pe.wait_ge(h2_kept, t + 1)
                    nc.tensor.matmul(dnn_ps[:, bass.ds(t, 1)], lhsT=h2[:], rhs=w3[:], start=True, stop=True
                                     ).then_inc(dnn_done, 1)

        @block.scalar
        def _(act):
            nc.scalar.preload_act_table(ACT.Sigmoid)
            act.dma_start(w2[:], W2).then_inc(small_loaded, 16)
            act.dma_start(w3[:], W3).then_inc(small_loaded, 16)
            act.dma_start(b1c[:], b1.unsqueeze(1)).then_inc(small_loaded, 16)
            act.dma_start(b2c[:], b2.unsqueeze(1)).then_inc(small_loaded, 16)
            act.dma_start(fm_bias_c, fm_bias.unsqueeze(0).broadcast_to([P, 1])).then_inc(small_loaded, 16)
            act.dma_start(b3_c, b3.unsqueeze(0).broadcast_to([P, 1])).then_inc(small_loaded, 16)
            act.dma_start(bf_c, bf.unsqueeze(0).broadcast_to([P, 1])).then_inc(small_loaded, 16)
            act.dma_start(scal[:, 3:5], Wf.rearrange("a b -> b a").broadcast_to([P, 2])).then_inc(small_loaded, 16)

            def set_defaults(k):
                nc.scalar.copy(placed[k][:], last_rows[:]).then_inc(defaults_set, 1)

            act.wait_ge(last_loaded, 16)
            set_defaults(0)
            set_defaults(1)
            act.wait_ge(small_loaded, 16 * 8)

            with act.Fori(0, TILES // 2) as pair:
                for k in range(2):
                    t = 2 * pair + k
                    act.wait_ge(fm_summed, 2 * t + 1)
                    nc.scalar.copy(dnn_in[k][:].rearrange("p (f e) -> p f e", e=E), placed[k][:, :, DNN]
                                   ).then_inc(dnn_in_made, 1)
                    nc.scalar.activation(square_sink[:], placed[k][:, :, FM], ACT.Square,
                                         accum_out=sum_of_sq[:, bass.ds(t, 1)]).then_inc(squared, 1)
                    act.wait_ge(transposed, t + 1)
                    nc.scalar.copy(dnn_t[k][:, 0:FULL, :], dnn_tp[k][:, 0:FULL, :]).then_inc(dnn_t_kept, 1)
                    nc.scalar.copy(dnn_t[k][0:REST, FULL, :], dnn_tp[k][0:REST, FULL, :]).then_inc(dnn_t_kept, 1)
                    act.wait_ge(h1_done, t + 1)
                    nc.scalar.activation(h1[:], h1_ps, ACT.Relu, bias=b1c[:, 0:1]).then_inc(h1_kept, 1)
                    act.wait_ge(h2_done, t + 1)
                    nc.scalar.activation(h2[:], h2_ps, ACT.Relu, bias=b2c[:, 0:1]).then_inc(h2_kept, 1)
                    act.wait_ge(fm_summed, 2 * (t + 1))
                    set_defaults(k)

            act.wait_ge(logit_done, 1)
            nc.scalar.activation(y[:], logit[:], ACT.Sigmoid).then_inc(y_done, 1)


_NAMES = ["r_idx", "rows", "fm_bias", "W1", "b1", "W2", "b2", "W3", "b3", "Wf", "bf"]


def kernel(**inputs):
    import numpy as np
    import concourse.bacc as bacc
    from concourse.bass_utils import run_bass_kernel_spmd

    given = {n: np.asarray(inputs[n if n == "r_idx" else "L0_rec_" + n]) for n in _NAMES if n != "rows"}
    dnn_emb, fm_emb, lin_w = (np.asarray(inputs["L0_rec_" + n]) for n in ("dnn_emb", "fm_emb", "lin_w"))
    F, V, E = dnn_emb.shape
    given["rows"] = np.concatenate([dnn_emb, fm_emb, lin_w[:, :, None]], axis=2).reshape(F * V, 2 * E + 1)
    given["fm_bias"] = given["fm_bias"].reshape(1)

    nc = bacc.Bacc("TRN2", target_bir_lowering=False, num_devices=1)
    arrays, args = {}, []
    for name in _NAMES:
        a = np.ascontiguousarray(given[name])
        arrays[f"in_{name}"] = a
        args.append(nc.dram_tensor(f"in_{name}", a.shape, mybir.dt.from_np(a.dtype), kind="ExternalInput").ap())
    B = given["r_idx"].shape[0]
    args.append(nc.dram_tensor("out", (B,), F32, kind="ExternalOutput").ap())
    deepfm_kernel(nc, *args, V)
    r = run_bass_kernel_spmd(nc, [arrays], core_ids=[0])
    return r.results[0]["out"]
```

```python
from contextlib import ExitStack

import concourse.bass as bass
from concourse import mybir

P = 128
F32 = mybir.dt.float32
I32 = mybir.dt.int32
U32 = mybir.dt.uint32
ALU = mybir.AluOpType
ACT = mybir.ActivationFunctionType
AX = mybir.AxisListType


def deepfm_kernel(nc, r_idx, rows_dram, fm_bias, W1, b1, W2, b2, W3, b3, Wf, bf, out, V):
    B, F = r_idx.shape
    ROW = rows_dram.shape[1]
    D1, D2 = W2.shape
    E = W1.shape[0] // F
    TILES = B // P
    DNN, FM, FM_LIN = slice(0, E), slice(E, 2 * E), slice(E, ROW)
    assert ROW == 2 * E + 1 and TILES % 2 == 0

    HEAD, STEP = 8, 1
    TAIL = F - HEAD
    SLAB = 32
    SLABS = P // SLAB
    assert F <= SLAB and TILES % SLABS == 0
    TERMS = E + 2
    ROUNDS = -(-F // 8)
    LIST = 8 * ROUNDS
    PER = P // E
    CHUNKS = [(f, min(PER, F - f)) for f in range(0, F, PER)]
    FULL = F // PER
    REST = (F - FULL * PER) * E
    assert len(CHUNKS) == FULL + 1

    with ExitStack() as ctx:
        def sb(name, shape, dt=F32):
            return ctx.enter_context(nc.sbuf_tensor(name, shape, dt))

        def bank(name, dt=F32):
            return ctx.enter_context(nc.psum_tensor(name, [P, 512], dt))

        def sem(name):
            return ctx.enter_context(nc.semaphore(name))

        field_base = sb("field_base", [P, F])
        ident = sb("ident", [P, P])
        last_dnn = sb("last_dnn", [P, F, E])
        last_terms = sb("last_terms", [P, SLABS, TERMS])
        last_square_sink = sb("last_square_sink", [P, E])
        w1 = sb("w1", [P, len(CHUNKS), D1])
        w2 = sb("w2", [D1, D2])
        w3 = sb("w3", [D2, 1])
        b1c = sb("b1c", [D1, 1])
        b2c = sb("b2c", [D2, 1])
        scal = sb("scal", [P, 5])
        fm_bias_c, b3_c, bf_c, wf0_c, wf1_c = (scal[:, i:i + 1] for i in range(5))
        const_c = sb("const_c", [P, 2])

        idx = sb("idx", [P, TILES, F], I32)
        capped = sb("capped", [P, TILES, F])
        wrap = sb("wrap", [P, TILES, F])
        value = sb("value", [P, TILES, F])
        listed = sb("listed", [P, TILES, F])
        at_last = sb("at_last", [P, TILES, SLAB])
        at_last_t = sb("at_last_t", [P, TILES // SLABS, P])
        key1 = sb("key1", [P, TILES, F])
        keys = sb("keys", [P, TILES + 1, F])
        length = sb("length", [P, TILES])
        longest = sb("longest", [TILES, 1])
        longest_row = sb("longest_row", [1, TILES])
        longest_i = sb("longest_i", [1, TILES], I32)
        assert TAIL % STEP == 0
        STEPS = TAIL // STEP
        step_start = sb("step_start", [1, STEPS])
        step_taken = sb("step_taken", [1, TILES, STEPS])
        steps_taken = sb("steps_taken", [1, TILES])
        steps_so_far = sb("steps_so_far", [1, TILES])
        no_steps = sb("no_steps", [1, TILES])
        tail_count = sb("tail_count", [1, TILES + 1], I32)
        work = [sb(f"work{i}", [P, F]) for i in range(2)]
        tile_keys = [sb(f"tile_keys{i}", [P, F]) for i in range(2)]
        top = sb("top", [P, LIST])
        entry_key = [sb(f"entry_key{i}", [P, LIST]) for i in range(2)]
        entry_row = [sb(f"entry_row{i}", [P, LIST], U32) for i in range(2)]

        packed = [sb(f"packed{i}", [P, F, ROW]) for i in range(2)]
        dnn_in = [sb(f"dnn_in{i}", [P, F, E]) for i in range(2)]
        tile_terms = [sb(f"tile_terms{i}", [P, TERMS]) for i in range(2)]
        square_sink = sb("square_sink", [P, F, E])
        dnn_t = [sb(f"dnn_t{i}", [P, len(CHUNKS), P]) for i in range(2)]
        h1 = sb("h1", [D1, P])
        h2 = sb("h2", [D2, P])

        packed_terms = sb("packed_terms", [P, TILES, TERMS])
        terms = sb("terms", [P, TILES, TERMS])
        fm_sum_sq = sb("fm_sum_sq", [P, TILES, E])
        sq_of_sum = sb("sq_of_sum", [P, TILES])
        pair_diff = sb("pair_diff", [P, TILES])
        fm_out = sb("fm_out", [P, TILES])
        dnn_part = sb("dnn_part", [P, TILES])
        logit = sb("logit", [P, TILES])
        y = sb("y", [P, TILES])

        HALF = F // 2
        match = [bank(f"match{i}", I32)[:, 0:HALF * F].rearrange("p (j f) -> p j f", f=F) for i in range(2)]
        late_match = bank("late_match", I32)[:, 0:HALF * HALF].rearrange("p (j f) -> p j f", f=HALF)
        dnn_tp = [bank(f"dnn_tp{i}")[:].rearrange("p (c b) -> p c b", b=P) for i in range(2)]
        last_share = bank("last_share")[:, 0:TILES * TERMS].rearrange("p (t n) -> p t n", n=TERMS)
        hidden_ps = bank("hidden_ps")
        h1_ps, h2_ps = hidden_ps[0:D1, 0:P], hidden_ps[0:D2, P:2 * P]
        ends_ps = bank("ends_ps")
        len_ps, dnn_ps = ends_ps[:, 0:P], ends_ps[:, P:P + TILES]
        mask_ps = dnn_tp[0]

        waits_over = sem("waits_over")
        idx_loaded = sem("idx_loaded")
        last_loaded = sem("last_loaded")
        w1_loaded = sem("w1_loaded")
        small_loaded = sem("small_loaded")
        base_made = sem("base_made")
        ident_made = sem("ident_made")
        key_step = sem("key_step")
        lengths_made = sem("lengths_made")
        lengths_t = sem("lengths_t")
        longest_made = sem("longest_made")
        longest_t = sem("longest_t")
        longest_known = sem("longest_known")
        list_step = sem("list_step")
        list_made = sem("list_made")
        head_landed = sem("head_landed")
        tail_landed = sem("tail_landed")
        entry_placed = sem("entry_placed")
        late_match_made = sem("late_match_made")
        match_made = sem("match_made")
        head_over = sem("head_over")
        tail_over = sem("tail_over")
        last_terms_cleared = sem("last_terms_cleared")
        at_last_cleared = sem("at_last_cleared")
        last_terms_made = sem("last_terms_made")
        at_last_made = sem("at_last_made")
        mask_t = sem("mask_t")
        mask_t_kept = sem("mask_t_kept")
        last_share_made = sem("last_share_made")
        defaults_set = sem("defaults_set")
        dnn_in_made = sem("dnn_in_made")
        tile_summed = sem("tile_summed")
        terms_kept = sem("terms_kept")
        transposed = sem("transposed")
        dnn_t_kept = sem("dnn_t_kept")
        h1_done = sem("h1_done")
        h1_kept = sem("h1_kept")
        h2_done = sem("h2_done")
        h2_kept = sem("h2_kept")
        dnn_done = sem("dnn_done")
        const_step = sem("const_step")
        end_step = sem("end_step")
        logit_done = sem("logit_done")
        y_done = sem("y_done")
        stored = sem("stored")

        def wait_alone(eng, semaphore, count):
            eng.wait_ge(semaphore, count)
            eng.sem_inc(waits_over, 1)

        block = ctx.enter_context(nc.Block())

        @block.sync
        def _(sp):
            sp.dma_start(idx[:], r_idx.rearrange("(p t) f -> p t f", p=P)).then_inc(idx_loaded, 16)
            last = rows_dram[1:F * V + 1, :].rearrange("(f v) r -> f v r", v=V)[:, V - 1, :]
            sp.wait_ge(last_terms_cleared, 1)
            for q in range(SLABS):
                sp.dma_start(last_terms[q * SLAB:q * SLAB + F, q, 0:E + 1], last[:, FM_LIN]).then_inc(last_loaded, 16)
            sp.dma_start(last_dnn[:], last[:, DNN].unsqueeze(0).broadcast_to([P, F, E])).then_inc(last_loaded, 16)
            sp.dma_start(w1[:, 0:FULL, :], W1[0:FULL * P, :].rearrange("(c k) n -> k c n", k=P)
                         ).then_inc(w1_loaded, 16)
            sp.dma_start(w1[0:REST, FULL, :], W1[FULL * P:FULL * P + REST, :]).then_inc(w1_loaded, 16)
            sp.wait_ge(y_done, 1)
            sp.dma_start(out.rearrange("(p t) -> p t", p=P), y[:]).then_inc(stored, 16)
            sp.wait_ge(stored, 16)

        @block.gpsimd
        def _(pool):
            nc.gpsimd.iota(step_start[:], [[STEP, STEPS]], base=HEAD, channel_multiplier=0,
                           allow_small_or_imprecise_dtypes=True)
            nc.gpsimd.iota(field_base[:], [[V, F]], base=2, channel_multiplier=0,
                           allow_small_or_imprecise_dtypes=True).then_inc(base_made, 1)
            nc.gpsimd.memset(ident[:], 0.0).then_inc(ident_made, 1)
            pool.wait_ge(ident_made, 1)
            nc.gpsimd.affine_select(out=ident[:], in_=ident[:], compare_op=ALU.not_equal, fill=1.0, base=0,
                                    pattern=[[-1, P]], channel_multiplier=1).then_inc(ident_made, 1)

            def fetch(k, j, landed):
                nc.gpsimd.indirect_dma_start(
                    out=packed[k][:, j, :], out_offset=None, in_=rows_dram,
                    in_offset=bass.IndirectOffsetOnAxis(ap=entry_row[k][:, j:j + 1], axis=0),
                ).then_inc(landed, 16)

            def fetch_tail(k, j, n):
                with pool.If(n > j):
                    for i in range(j, min(j + STEP, F)):
                        fetch(k, i, tail_landed)
                    if j + STEP < F:
                        fetch_tail(k, j + STEP, n)

            with pool.Fori(0, TILES // 2) as pair:
                for k in range(2):
                    t = 2 * pair + k
                    wait_alone(pool, head_over, t + 1)
                    wait_alone(pool, list_made, t + 1)
                    for j in range(HEAD):
                        fetch(k, j, head_landed)
                    pool.wait_ge(longest_known, 2)
                    n = pool.value_load(longest_i[0:1, bass.ds(t, 1)], min_val=0, max_val=F)
                    wait_alone(pool, tail_over, t + 1)
                    fetch_tail(k, HEAD, n)

        @block.vector
        def _(dve):
            steps = [0]

            def key_made(ins):
                ins.then_inc(key_step, 1)
                steps[0] += 1
                dve.wait_ge(key_step, steps[0])

            dve.sem_inc(head_over, 1)
            dve.sem_inc(tail_over, 1)
            nc.vector.memset(last_terms[:], 0.0).then_inc(last_terms_cleared, 1)
            nc.vector.memset(at_last[:], 0.0).then_inc(at_last_cleared, 1)
            nc.vector.memset(keys[:, TILES, :], 0.0)
            dve.wait_ge(idx_loaded, 16)
            key_made(nc.vector.tensor_scalar(capped[:], idx[:], float(V - 1), float(-V), ALU.min, ALU.max))
            key_made(nc.vector.tensor_scalar(wrap[:], capped[:], 0.0, float(V), ALU.is_lt, ALU.mult))
            key_made(nc.vector.tensor_tensor(value[:], capped[:], wrap[:], ALU.add))
            nc.vector.tensor_scalar(listed[:], value[:], float(V - 1), None, ALU.is_lt)
            dve.wait_ge(base_made, 1)
            key_made(nc.vector.tensor_tensor(key1[:], value[:],
                                             field_base[:].unsqueeze(1).broadcast_to([P, TILES, F]), ALU.add))
            dve.wait_ge(at_last_cleared, 1)
            nc.vector.tensor_scalar(at_last[:, :, 0:F], value[:], float(V - 1), None, ALU.is_equal).then_inc(at_last_made, 1)
            key_made(nc.vector.tensor_tensor(keys[:, 0:TILES, :], key1[:], listed[:], ALU.mult))

            def make_list(k, t):
                dve.sem_clear(list_step)
                done = [0]

                def made(ins):
                    ins.then_inc(list_step, 1)
                    done[0] += 1
                    dve.wait_ge(list_step, done[0])

                made(nc.vector.tensor_copy(tile_keys[k][:], keys[:, bass.ds(t, 1), :].rearrange("p o f -> p (o f)")))
                src = tile_keys[k]
                for r in range(ROUNDS):
                    eight = top[:, 8 * r:8 * r + 8]
                    made(nc.vector.max(eight, src[:]))
                    if r + 1 < ROUNDS:
                        made(nc.vector.match_replace(work[r % 2][:], eight, src[:], 0.0))
                        src = work[r % 2]
                made(nc.vector.tensor_scalar(entry_key[k][:], top[:], 1.0, None, ALU.max))
                nc.vector.tensor_scalar(entry_row[k][:], entry_key[k][:], -1.0, None, ALU.add).then_inc(list_made, 1)
                nc.vector.tensor_tensor(match[k],
                                        tile_keys[k][:].unsqueeze(1).broadcast_to([P, HALF, F]),
                                        entry_key[k][:, 0:HALF].unsqueeze(2).broadcast_to([P, HALF, F]),
                                        ALU.is_equal).then_inc(match_made, 1)

            def place(k, j):
                m = F - j
                hit = match[k][:, j, 0:m] if j < HALF else late_match[:, j - HALF, 0:m]
                if j:
                    dve.wait_ge(entry_placed, j)
                nc.vector.copy_predicated(
                    dnn_in[k][:, 0:m, :],
                    hit.unsqueeze(2).broadcast_to([P, m, E]),
                    packed[k][:, j, DNN].unsqueeze(1).broadcast_to([P, m, E])).then_inc(entry_placed, 1)

            def sum_up(k, m):
                dve.wait_ge(entry_placed, m)
                nc.vector.tensor_reduce(tile_terms[k][:, 0:E + 1],
                                        packed[k][:, 0:m, FM_LIN].rearrange("p j e -> p e j"),
                                        AX.X, ALU.add).then_inc(tile_summed, 1)
                nc.vector.tensor_tensor_reduce(out=square_sink[:, 0:m, :], in0=packed[k][:, 0:m, FM],
                                               in1=packed[k][:, 0:m, FM], scale=1.0, scalar=0.0,
                                               op0=ALU.mult, op1=ALU.add,
                                               accum_out=tile_terms[k][:, E + 1:TERMS]).then_inc(tile_summed, 1)

            def place_tail(k, j, n):
                with dve.If(n > j):
                    if j == HALF:
                        nc.vector.tensor_tensor(late_match,
                                                tile_keys[k][:, 0:HALF].unsqueeze(1).broadcast_to([P, HALF, HALF]),
                                                entry_key[k][:, HALF:F].unsqueeze(2).broadcast_to([P, HALF, HALF]),
                                                ALU.is_equal).then_inc(late_match_made, 1)
                        dve.wait_ge(late_match_made, 1)
                        dve.sem_clear(late_match_made)
                    for i in range(j, j + STEP):
                        place(k, i)
                    if j + STEP < F:
                        place_tail(k, j + STEP, n)
                    else:
                        sum_up(k, F)
                with dve.Else():
                    sum_up(k, j)

            make_list(0, 0)
            nc.vector.tensor_reduce(length[:], listed[:], AX.X, ALU.add).then_inc(lengths_made, 1)
            dve.wait_ge(lengths_t, 1)
            nc.vector.tensor_reduce(longest[:], len_ps[0:TILES, :], AX.X, ALU.max).then_inc(longest_made, 1)
            dve.wait_ge(longest_t, 1)
            nc.vector.tensor_copy(longest_i[:], len_ps[0:1, 0:TILES]).then_inc(longest_known, 1)
            nc.vector.memset(no_steps[:], 0.0)
            nc.vector.memset(tail_count[:], 0)
            key_made(nc.vector.tensor_copy(longest_row[:], len_ps[0:1, 0:TILES]))
            key_made(nc.vector.tensor_tensor(step_taken[:],
                                             longest_row[:].unsqueeze(2).broadcast_to([1, TILES, STEPS]),
                                             step_start[:].unsqueeze(1).broadcast_to([1, TILES, STEPS]), ALU.is_gt))
            key_made(nc.vector.tensor_reduce(steps_taken[:], step_taken[:], AX.X, ALU.add))
            key_made(nc.vector.tensor_tensor_scan(steps_so_far[:], steps_taken[:], no_steps[:], 0.0, ALU.add, ALU.add))
            nc.vector.tensor_scalar(tail_count[:, 1:TILES + 1], steps_so_far[:], 16.0 * STEP, None, ALU.mult
                                    ).then_inc(longest_known, 1)

            dve.wait_ge(small_loaded, 16 * 8)
            nc.vector.tensor_scalar(const_c[:, 0:1], b3_c, wf1_c, bf_c, ALU.mult, ALU.add).then_inc(const_step, 1)
            dve.wait_ge(const_step, 1)
            nc.vector.tensor_scalar(const_c[:, 1:2], fm_bias_c, wf0_c, const_c[:, 0:1], ALU.mult, ALU.add
                                    ).then_inc(const_step, 1)
            dve.wait_ge(longest_known, 2)

            with dve.Fori(0, TILES // 2) as pair:
                for k in range(2):
                    t = 2 * pair + k
                    make_list(1 - k, t + 1)
                    n = dve.value_load(longest_i[0:1, bass.ds(t, 1)], min_val=0, max_val=F)
                    after = dve.value_load(tail_count[0:1, bass.ds(t + 1, 1)], min_val=0, max_val=16 * TAIL * TILES)
                    wait_alone(dve, match_made, t + 1)
                    wait_alone(dve, defaults_set, t + 1)
                    dve.sem_clear(entry_placed)
                    dve.wait_ge(head_landed, 16 * HEAD * (t + 1))
                    dve.sem_inc(head_over, 1)
                    for j in range(HEAD):
                        place(k, j)
                    with dve.If(n > HEAD):
                        dve.wait_ge(tail_landed, after)
                        dve.sem_inc(tail_over, 1)
                    with dve.Else():
                        dve.sem_inc(tail_over, 1)
                    wait_alone(dve, terms_kept, t + 1)
                    place_tail(k, HEAD, n)

            def ended(n, ins):
                ins.then_inc(end_step, 1)
                dve.wait_ge(end_step, n)

            dve.wait_ge(terms_kept, TILES + 2)
            dve.wait_ge(last_share_made, 1)
            ended(1, nc.vector.tensor_tensor(terms[:], packed_terms[:], last_share, ALU.add))
            ended(2, nc.vector.tensor_tensor(fm_sum_sq[:], terms[:, :, 0:E], terms[:, :, 0:E], ALU.mult))
            ended(3, nc.vector.tensor_reduce(sq_of_sum[:], fm_sum_sq[:], AX.X, ALU.add))
            ended(4, nc.vector.tensor_tensor(pair_diff[:], sq_of_sum[:], terms[:, :, E + 1], ALU.subtract))
            ended(5, nc.vector.scalar_tensor_tensor(out=fm_out[:], in0=pair_diff[:], scalar=0.5, in1=terms[:, :, E],
                                                    op0=ALU.mult, op1=ALU.add))
            dve.wait_ge(const_step, 2)
            dve.wait_ge(dnn_done, TILES)
            ended(6, nc.vector.tensor_scalar(dnn_part[:], dnn_ps, wf1_c, const_c[:, 1:2], ALU.mult, ALU.add))
            nc.vector.scalar_tensor_tensor(out=logit[:], in0=fm_out[:], scalar=wf0_c, in1=dnn_part[:],
                                           op0=ALU.mult, op1=ALU.add).then_inc(logit_done, 1)

        @block.tensor
        def _(pe):
            pe.wait_ge(ident_made, 2)
            pe.wait_ge(lengths_made, 1)
            nc.tensor.transpose(len_ps[0:TILES, :], length[:], ident[:]).then_inc(lengths_t, 1)
            pe.wait_ge(longest_made, 1)
            nc.tensor.transpose(len_ps[0:1, 0:TILES], longest[:], ident[0:TILES, 0:TILES]).then_inc(longest_t, 1)
            pe.wait_ge(at_last_made, 1)
            for g in range(TILES // SLABS):
                last = nc.tensor.transpose(mask_ps[:, g, :],
                                           at_last[:, g * SLABS:(g + 1) * SLABS, :].rearrange("p t f -> p (t f)"),
                                           ident[:])
            last.then_inc(mask_t, 1)
            pe.wait_ge(last_terms_made, SLABS)
            pe.wait_ge(mask_t_kept, 1)
            for g in range(TILES // SLABS):
                last = nc.tensor.matmul(last_share[:, g * SLABS:(g + 1) * SLABS, :].rearrange("p t n -> p (t n)"),
                                        lhsT=at_last_t[:, g, :], rhs=last_terms[:].rearrange("p q n -> p (q n)"),
                                        start=True, stop=True)
            last.then_inc(last_share_made, 1)
            pe.wait_ge(w1_loaded, 32)
            pe.wait_ge(small_loaded, 16 * 8)

            with pe.Fori(0, TILES // 2) as pair:
                for k in range(2):
                    t = 2 * pair + k
                    pe.wait_ge(tile_summed, 2 * t + 1)
                    for c, (f, n) in enumerate(CHUNKS):
                        last = nc.tensor.transpose(dnn_tp[k][0:n * E, c, :], dnn_in[k][:, f:f + n, :].rearrange("p f e -> p (f e)"), ident[:])
                    last.then_inc(transposed, 1)
                    pe.wait_ge(dnn_t_kept, 2 * (t + 1))
                    for c, (f, n) in enumerate(CHUNKS):
                        last = nc.tensor.matmul(h1_ps, lhsT=w1[0:n * E, c, :], rhs=dnn_t[k][0:n * E, c, :],
                                                start=c == 0, stop=c == FULL)
                    last.then_inc(h1_done, 1)
                    wait_alone(pe, h1_kept, t + 1)
                    nc.tensor.matmul(h2_ps, lhsT=w2[:], rhs=h1[:], start=True, stop=True).then_inc(h2_done, 1)
                    pe.wait_ge(h2_kept, t + 1)
                    nc.tensor.matmul(dnn_ps[:, bass.ds(t, 1)], lhsT=h2[:], rhs=w3[:], start=True, stop=True
                                     ).then_inc(dnn_done, 1)

        @block.scalar
        def _(act):
            nc.scalar.preload_act_table(ACT.Sigmoid)
            act.dma_start(w2[:], W2).then_inc(small_loaded, 16)
            act.dma_start(w3[:], W3).then_inc(small_loaded, 16)
            act.dma_start(b1c[:], b1.unsqueeze(1)).then_inc(small_loaded, 16)
            act.dma_start(b2c[:], b2.unsqueeze(1)).then_inc(small_loaded, 16)
            act.dma_start(fm_bias_c, fm_bias.unsqueeze(0).broadcast_to([P, 1])).then_inc(small_loaded, 16)
            act.dma_start(b3_c, b3.unsqueeze(0).broadcast_to([P, 1])).then_inc(small_loaded, 16)
            act.dma_start(bf_c, bf.unsqueeze(0).broadcast_to([P, 1])).then_inc(small_loaded, 16)
            act.dma_start(scal[:, 3:5], Wf.rearrange("a b -> b a").broadcast_to([P, 2])).then_inc(small_loaded, 16)

            def set_defaults(k):
                nc.scalar.copy(dnn_in[k][:], last_dnn[:]).then_inc(defaults_set, 1)

            act.wait_ge(last_loaded, 16 * (SLABS + 1))
            set_defaults(0)
            set_defaults(1)
            for q in range(SLABS):
                fields = slice(q * SLAB, q * SLAB + F)
                nc.scalar.activation(last_square_sink[fields, :], last_terms[fields, q, 0:E], ACT.Square,
                                     accum_out=last_terms[fields, q, E + 1:TERMS]).then_inc(last_terms_made, 1)
            act.sem_inc(terms_kept, 2)
            act.wait_ge(mask_t, 1)
            nc.scalar.copy(at_last_t[:], mask_ps).then_inc(mask_t_kept, 1)
            act.wait_ge(small_loaded, 16 * 8)

            with act.Fori(0, TILES // 2) as pair:
                for k in range(2):
                    t = 2 * pair + k
                    act.wait_ge(transposed, t + 1)
                    nc.scalar.copy(dnn_t[k][:, 0:FULL, :], dnn_tp[k][:, 0:FULL, :]).then_inc(dnn_t_kept, 1)
                    nc.scalar.copy(dnn_t[k][0:REST, FULL, :], dnn_tp[k][0:REST, FULL, :]).then_inc(dnn_t_kept, 1)
                    set_defaults(k)
                    act.wait_ge(tile_summed, 2 * (t + 1))
                    nc.scalar.copy(packed_terms[:, bass.ds(t, 1), :], tile_terms[k][:].unsqueeze(1)
                                   ).then_inc(terms_kept, 1)
                    act.wait_ge(h1_done, t + 1)
                    nc.scalar.activation(h1[:], h1_ps, ACT.Relu, bias=b1c[:, 0:1]).then_inc(h1_kept, 1)
                    act.wait_ge(h2_done, t + 1)
                    nc.scalar.activation(h2[:], h2_ps, ACT.Relu, bias=b2c[:, 0:1]).then_inc(h2_kept, 1)

            act.wait_ge(logit_done, 1)
            nc.scalar.activation(y[:], logit[:], ACT.Sigmoid).then_inc(y_done, 1)


_NAMES = ["r_idx", "rows", "fm_bias", "W1", "b1", "W2", "b2", "W3", "b3", "Wf", "bf"]


def kernel(**inputs):
    import numpy as np
    import concourse.bacc as bacc
    from concourse.bass_utils import run_bass_kernel_spmd

    given = {n: np.asarray(inputs[n if n == "r_idx" else "L0_rec_" + n]) for n in _NAMES if n != "rows"}
    dnn_emb, fm_emb, lin_w = (np.asarray(inputs["L0_rec_" + n]) for n in ("dnn_emb", "fm_emb", "lin_w"))
    F, V, E = dnn_emb.shape
    rows = np.zeros((1 + F * V, 2 * E + 1), dnn_emb.dtype)
    rows[1:] = np.concatenate([dnn_emb, fm_emb, lin_w[:, :, None]], axis=2).reshape(F * V, 2 * E + 1)
    given["rows"] = rows
    given["fm_bias"] = given["fm_bias"].reshape(1)

    nc = bacc.Bacc("TRN2", target_bir_lowering=False, num_devices=1)
    arrays, args = {}, []
    for name in _NAMES:
        a = np.ascontiguousarray(given[name])
        arrays[f"in_{name}"] = a
        args.append(nc.dram_tensor(f"in_{name}", a.shape, mybir.dt.from_np(a.dtype), kind="ExternalInput").ap())
    B = given["r_idx"].shape[0]
    args.append(nc.dram_tensor("out", (B,), F32, kind="ExternalOutput").ap())
    deepfm_kernel(nc, *args, V)
    r = run_bass_kernel_spmd(nc, [arrays], core_ids=[0])
    return r.results[0]["out"]
```

```python
from contextlib import ExitStack

import concourse.bass as bass
from concourse import mybir

P = 128
F32 = mybir.dt.float32
I32 = mybir.dt.int32
U32 = mybir.dt.uint32
ALU = mybir.AluOpType
ACT = mybir.ActivationFunctionType
AX = mybir.AxisListType


def deepfm_kernel(nc, r_idx, rows_dram, fm_bias, W1, b1, W2, b2, W3, b3, Wf, bf, out, V, DIRECT):
    B, F = r_idx.shape
    ROW = rows_dram.shape[1]
    D1, D2 = W2.shape
    E = W1.shape[0] // F
    TILES = B // P
    DNN, FM, FM_LIN = slice(0, E), slice(E, 2 * E), slice(E, ROW)
    TERMS = E + 2
    assert ROW == 2 * E + 1

    S = F - DIRECT
    GROUP = 4
    SPAN = 2 * GROUP
    GROUPS, PAIRS = TILES // GROUP, TILES // SPAN
    TOP = 8
    HEAD = 3
    REACH = S - HEAD
    ROUND = 2 * TOP
    ROUNDS = -(-GROUP * REACH // ROUND)
    FIRST_OVER = 2
    BACK_TILE = GROUP
    NEXT_OVER = SPAN - 1
    STRIDE_BITS = (F * V).bit_length()
    STRIDE = 1 << STRIDE_BITS
    assert TILES % SPAN == 0 and (GROUP + 1 + ROUND) * STRIDE <= 1 << 24
    assert ROUND <= REACH
    RIGHT_SHIFT = ROUND.bit_length() - 1
    assert ROUND == 1 << RIGHT_SHIFT

    PER = P // E
    CHUNKS = [(f, min(PER, S - f)) for f in range(0, S, PER)] + [(S, DIRECT)]
    FULL = S // PER
    REST = (S - FULL * PER) * E
    SLAB = 32
    assert len(CHUNKS) == FULL + 2 and DIRECT <= PER and S <= SLAB and GROUP * SLAB == P

    with ExitStack() as ctx:
        def sb(name, shape, dt=F32):
            return ctx.enter_context(nc.sbuf_tensor(name, shape, dt))

        def bank(name, dt=F32):
            return ctx.enter_context(nc.psum_tensor(name, [P, 512], dt))

        def sem(name):
            return ctx.enter_context(nc.semaphore(name))

        key_base = sb("key_base", [P, GROUP, F])
        tile_no = sb("tile_no", [P, GROUP])
        ident = sb("ident", [P, P])
        last_dnn = sb("last_dnn", [P, S, E])
        last_terms = sb("last_terms", [P, GROUP, TERMS])
        last_square_sink = sb("last_square_sink", [P, E])
        w1 = sb("w1", [P, len(CHUNKS), D1])
        w2 = sb("w2", [D1, D2])
        w3 = sb("w3", [D2, 1])
        b1c = sb("b1c", [D1, 1])
        b2c = sb("b2c", [D2, 1])
        scal = sb("scal", [P, 5])
        fm_bias_c, b3_c, bf_c, wf0_c, wf1_c = (scal[:, i:i + 1] for i in range(5))
        const_c = sb("const_c", [P, 2])

        idx = sb("idx", [P, TILES, F], I32)
        capped = sb("capped", [P, TILES, F])
        wrap = sb("wrap", [P, TILES, F])
        value = sb("value", [P, TILES, F])
        based = sb("based", [P, TILES, F])
        direct_rows = sb("direct_rows", [P, TILES + SPAN, DIRECT], U32)
        keys = sb("keys", [P, TILES + SPAN, S])
        at_last = sb("at_last", [P, TILES, SLAB])
        at_last_t = sb("at_last_t", [P, GROUPS, P])
        last_count = sb("last_count", [P, TILES])
        beyond = sb("beyond", [P, TILES])
        left = sb("left", [P, TILES])
        over_length = sb("over_length", [P, GROUPS + PAIRS])
        longest = sb("longest", [GROUPS + PAIRS, 1])
        longest_row = sb("longest_row", [1, GROUPS + PAIRS])
        slot_no = sb("slot_no", [P, REACH])
        filler = sb("filler", [P, REACH])
        free_slots = sb("free_slots", [P, GROUPS])
        fillers = sb("fillers", [P, PAIRS + 1, REACH])
        fits = sb("fits", [1, PAIRS])
        slots = sb("slots", [1, PAIRS])
        slots_so_far = sb("slots_so_far", [1, PAIRS])
        slots_i = sb("slots_i", [1, PAIRS + 1], I32)
        target_i = sb("target_i", [1, PAIRS], I32)
        start_i = sb("start_i", [1, PAIRS], I32)
        room_i = sb("room_i", [1, PAIRS + 1], I32)
        shared = sb("shared", [1, GROUPS])
        extra = sb("extra", [1, GROUPS])
        shared_i = sb("shared_i", [1, GROUPS], I32)
        extra_i = sb("extra_i", [1, GROUPS], I32)
        shift_i = sb("shift_i", [1, GROUPS], I32)
        extra_up = sb("extra_up", [1, GROUPS], U32)
        rounds_i = sb("rounds_i", [1, GROUPS], U32)
        rounds = sb("rounds", [1, GROUPS])
        rounds_so_far = sb("rounds_so_far", [1, GROUPS])
        rounds_before = sb("rounds_before", [1, GROUPS])
        before_i = sb("before_i", [1, GROUPS], I32)
        zeros_row = sb("zeros_row", [1, GROUPS])

        tile_keys = sb("tile_keys", [P, SPAN, S])
        top = sb("top", [P, SPAN, TOP])
        entry_key = sb("entry_key", [P, SPAN, TOP])
        entry_row = sb("entry_row", [P, SPAN, HEAD], U32)
        direct_based = sb("direct_based", [P, GROUP, DIRECT])
        direct_row = sb("direct_row", [P, SPAN, DIRECT], U32)
        packed = sb("packed", [P, SPAN, HEAD + DIRECT, ROW])
        dnn_in = sb("dnn_in", [P, SPAN, F, E])
        tile_squares = sb("tile_squares", [P, SPAN])
        square_sink = sb("square_sink", [P, HEAD + DIRECT, E])

        KEYS, TOPS = (GROUP + 1) * S, 2 * ROUND
        over_now = sb("over_now", [P, 2, 2 * KEYS + TOPS])
        over_next = sb("over_next", [P, 2, 2 * KEYS + TOPS])

        def over_views(buffer):
            return (buffer[:, :, 0:KEYS].rearrange("p s (q f) -> p s q f", f=S),
                    buffer[:, :, KEYS:2 * KEYS].rearrange("p s (q f) -> p s q f", f=S), buffer[:, :, 2 * KEYS:])

        now, ahead = over_views(over_now), over_views(over_next)
        next_top_i = sb("next_top_i", [P, 2, ROUND], U32)
        next_row = sb("next_row", [P, 2, TOPS], U32)
        next_over_row = sb("next_over_row", [P, ROUND], U32)
        over_row = sb("over_row", [P, ROUND], U32)
        extra_top_i = sb("extra_top_i", [P, ROUND], U32)
        extra_row = sb("extra_row", [P, ROUND], U32)
        over_packed = sb("over_packed", [P, 2 * ROUND, ROW])
        work_key = sb("work_key", [P, ROUND])
        work_top_i = sb("work_top_i", [P, ROUND], U32)
        work_tile = sb("work_tile", [P, ROUND], U32)
        work_of = sb("work_of", [P, GROUP, ROUND])
        work_rows = sb("work_rows", [P, ROUND, ROW + 1])
        over_squares = sb("over_squares", [P, ROUND, E])
        over_split = sb("over_split", [P, GROUP, TERMS, ROUND])
        round_terms = sb("round_terms", [P, GROUP, TERMS])

        dnn_t = [sb(f"dnn_t{i}", [P, len(CHUNKS), P]) for i in range(2)]
        h1 = sb("h1", [D1, P])
        h2 = sb("h2", [D2, P])

        head_terms = sb("head_terms", [P, TILES, TERMS])
        all_over_terms = sb("all_over_terms", [P, TILES, TERMS])
        last_share = sb("last_share", [P, TILES, TERMS])
        fetched_terms = sb("fetched_terms", [P, TILES, TERMS])
        terms = sb("terms", [P, TILES, TERMS])
        fm_sum_sq = sb("fm_sum_sq", [P, TILES, E])
        sq_of_sum = sb("sq_of_sum", [P, TILES])
        pair_diff = sb("pair_diff", [P, TILES])
        fm_out = sb("fm_out", [P, TILES])
        fm_part = sb("fm_part", [P, TILES])
        logit = sb("logit", [P, TILES])
        y = sb("y", [P, TILES])

        match_banks = [bank(f"match{i}", I32)[:, 0:GROUP * HEAD * S].rearrange("p (q j f) -> p q j f", j=HEAD, f=S)
                       for i in range(2)]
        match = [match_banks[q // GROUP][:, q % GROUP] for q in range(SPAN)]
        over_match = bank("over_match", I32)[:, 0:3 * GROUP * REACH].rearrange("p (i q f) -> p i q f", q=GROUP, f=REACH)
        dnn_tp = [bank(f"dnn_tp{i}")[:].rearrange("p (c b) -> p c b", b=P) for i in range(2)]
        mask_ps = bank("mask_ps")[:].rearrange("p (c b) -> p c b", b=P)
        h1_ps = bank("h1_ps")[0:D1, 0:P]
        h2_ps = mask_ps[0:D2, 0, :]
        ends_ps = bank("ends_ps")
        len_ps, dnn_ps = ends_ps[:, 0:P], ends_ps[:, P:P + TILES]
        direct_tp = len_ps
        share_ps = ends_ps[:, P + TILES:P + TILES + TILES * TERMS].rearrange("p (t n) -> p t n", n=TERMS)

        waits_over = sem("waits_over")
        idx_loaded = sem("idx_loaded")
        last_loaded = sem("last_loaded")
        w1_loaded = sem("w1_loaded")
        small_loaded = sem("small_loaded")
        base_made = sem("base_made")
        ident_made = sem("ident_made")
        cleared = sem("cleared")
        key_step = sem("key_step")
        at_last_made = sem("at_last_made")
        lengths_made = sem("lengths_made")
        lengths_t = sem("lengths_t")
        longest_made = sem("longest_made")
        longest_t = sem("longest_t")
        over_known = sem("over_known")
        last_terms_made = sem("last_terms_made")
        mask_t = sem("mask_t")
        mask_t_kept = sem("mask_t_kept")
        share_made = sem("share_made")
        share_kept = sem("share_kept")
        const_step = sem("const_step")
        pair_step = sem("pair_step")
        list_made = sem("list_made")
        list_step = sem("list_step")
        over_list_made = sem("over_list_made")
        extra_list_made = sem("extra_list_made")
        direct_made = sem("direct_made")
        head_landed = [sem(f"head_landed{q}") for q in range(SPAN)]
        direct_landed = [sem(f"direct_landed{q}") for q in range(SPAN)]
        direct_put = sem("direct_put")
        over_landed = sem("over_landed")
        extra_landed = sem("extra_landed")
        over_placed = sem("over_placed")
        over_step = sem("over_step")
        defaults_set = sem("defaults_set")
        tile_placed = sem("tile_placed")
        transposed = sem("transposed")
        direct_transposed = sem("direct_transposed")
        dnn_t_kept = sem("dnn_t_kept")
        h1_done = sem("h1_done")
        h1_kept = sem("h1_kept")
        h2_done = sem("h2_done")
        h2_kept = sem("h2_kept")
        dnn_done = sem("dnn_done")
        end_step = sem("end_step")
        logit_done = sem("logit_done")
        y_done = sem("y_done")
        stored = sem("stored")

        def wait_alone(eng, semaphore, count):
            eng.wait_ge(semaphore, count)
            eng.sem_inc(waits_over, 1)

        block = ctx.enter_context(nc.Block())

        @block.sync
        def _(sp):
            sp.dma_start(idx[:], r_idx.rearrange("(p t) f -> p t f", p=P)).then_inc(idx_loaded, 16)
            last = rows_dram[1:F * V + 1, :].rearrange("(f v) r -> f v r", v=V)[:, V - 1, :]
            sp.dma_start(last_dnn[:], last[0:S, DNN].unsqueeze(0).broadcast_to([P, S, E])).then_inc(last_loaded, 16)
            sp.wait_ge(cleared, 1)
            for q in range(GROUP):
                sp.dma_start(last_terms[q * SLAB:q * SLAB + S, q, 0:E + 1], last[0:S, FM_LIN]).then_inc(last_loaded, 16)
            sp.dma_start(w1[:, 0:FULL, :], W1[0:FULL * P, :].rearrange("(c k) n -> k c n", k=P)
                         ).then_inc(w1_loaded, 16)
            sp.dma_start(w1[0:REST, FULL, :], W1[FULL * P:S * E, :]).then_inc(w1_loaded, 16)
            sp.dma_start(w1[0:DIRECT * E, FULL + 1, :], W1[S * E:F * E, :]).then_inc(w1_loaded, 16)
            sp.wait_ge(y_done, 1)
            sp.dma_start(out.rearrange("(p t) -> p t", p=P), y[:]).then_inc(stored, 16)
            sp.wait_ge(stored, 16)

        @block.gpsimd
        def _(pool):
            for q in range(GROUP):
                nc.gpsimd.iota(key_base[:, q, 0:S], [[V, S]], base=1 + (q + 1) * STRIDE, channel_multiplier=0,
                               allow_small_or_imprecise_dtypes=True).then_inc(base_made, 1)
            nc.gpsimd.iota(key_base[:, :, S:F], [[0, GROUP], [V, DIRECT]], base=1 + S * V, channel_multiplier=0,
                           allow_small_or_imprecise_dtypes=True).then_inc(base_made, 1)
            nc.gpsimd.iota(slot_no[:], [[1, REACH]], base=0, channel_multiplier=0,
                           allow_small_or_imprecise_dtypes=True).then_inc(base_made, 1)
            nc.gpsimd.iota(tile_no[:], [[1, GROUP]], base=1, channel_multiplier=0,
                           allow_small_or_imprecise_dtypes=True).then_inc(base_made, 1)
            nc.gpsimd.memset(ident[:], 0.0).then_inc(ident_made, 1)
            pool.wait_ge(ident_made, 1)
            nc.gpsimd.affine_select(out=ident[:], in_=ident[:], compare_op=ALU.not_equal, fill=1.0, base=0,
                                    pattern=[[-1, P]], channel_multiplier=1).then_inc(ident_made, 1)

            def fetch(rows, numbers, semaphore):
                nc.gpsimd.indirect_dma_start(out=rows, out_offset=None, in_=rows_dram,
                                             in_offset=bass.IndirectOffsetOnAxis(ap=numbers, axis=0)
                                             ).then_inc(semaphore, 16)

            def fetch_head(pair, q):
                wait_alone(pool, list_made, SPAN * pair + q + 1)
                for j in range(HEAD):
                    fetch(packed[:, q, j, :], entry_row[:, q, j:j + 1], head_landed[q])

            def fetch_direct(pair, q):
                wait_alone(pool, direct_made, SPAN * pair + q + 1)
                for i in range(DIRECT):
                    fetch(packed[:, q, HEAD + i, :], direct_row[:, q, i:i + 1], direct_landed[q])

            def fetch_shared(j, n):
                with pool.If(n > j):
                    fetch(over_packed[:, j, :], over_row[:, j:j + 1], over_landed)
                    if j + 1 < ROUND:
                        fetch_shared(j + 1, n)

            def fetch_extra(group):
                n = pool.value_load(extra_i[0:1, bass.ds(group, 1)], min_val=0, max_val=GROUP * REACH)
                with pool.If(n > 0):
                    with pool.Fori(0, ROUNDS) as r:
                        with pool.If(n > r * ROUND):
                            pool.wait_ge(extra_list_made, 1)
                            pool.sem_clear(extra_list_made)
                            for j in range(ROUND):
                                fetch(over_packed[:, j, :], extra_row[:, j:j + 1], extra_landed)

            def fetch_overflow(pair):
                n = pool.value_load(slots_i[0:1, bass.ds(pair, 1)], min_val=0, max_val=ROUND)
                wait_alone(pool, over_list_made, pair + 1)
                fetch_shared(0, n)

            with pool.Fori(0, PAIRS) as pair:
                for q in range(SPAN):
                    if q == FIRST_OVER:
                        pool.wait_ge(over_known, 1)
                        with pool.If(pair < 1):
                            fetch_overflow(pair)
                        fetch_extra(2 * pair)
                    if q == BACK_TILE:
                        fetch_extra(2 * pair + 1)
                    if q == NEXT_OVER:
                        fetch_overflow(pair + 1)
                    if q == 0:
                        fetch_direct(pair, q)
                        fetch_head(pair, q)
                    else:
                        fetch_head(pair, q)
                        fetch_direct(pair, q)

        @block.vector
        def _(dve):
            steps = [0]

            def made(ins):
                ins.then_inc(key_step, 1)
                steps[0] += 1
                dve.wait_ge(key_step, steps[0])

            def cap(ts):
                return nc.vector.tensor_scalar(capped[:, ts], idx[:, ts], float(V - 1), float(-V), ALU.min, ALU.max)

            def make_wrap(ts):
                return nc.vector.tensor_scalar(wrap[:, ts], capped[:, ts], 0.0, float(V), ALU.is_lt, ALU.mult)

            def make_values(ts):
                return nc.vector.tensor_tensor(value[:, ts], capped[:, ts], wrap[:, ts], ALU.add)

            def make_based(ts, groups):
                return nc.vector.tensor_tensor(
                    based[:, ts].rearrange("p (g q) f -> p g (q f)", q=GROUP),
                    value[:, ts].rearrange("p (g q) f -> p g (q f)", q=GROUP),
                    key_base[:].rearrange("p q f -> p (q f)").unsqueeze(1).broadcast_to([P, groups, GROUP * F]),
                    ALU.add)

            def make_keys(ts):
                return nc.vector.scalar_tensor_tensor(out=keys[:, ts], in0=value[:, ts, 0:S], scalar=float(V - 1),
                                                      in1=based[:, ts, 0:S], op0=ALU.is_lt, op1=ALU.mult)

            def take_keys(pair):
                return nc.vector.tensor_copy(tile_keys[:], keys[:, bass.ds(SPAN * pair, SPAN), :])

            def find_top(q):
                return nc.vector.max(top[:, q, :], tile_keys[:, q, :])

            def make_entry_row(q):
                return nc.vector.tensor_scalar(entry_row[:, q, :], top[:, q, 0:HEAD], float(-(q % GROUP + 1) * STRIDE),
                                               0.0, ALU.add, ALU.max)

            def make_entry_keys(q0, q1):
                return nc.vector.tensor_scalar(entry_key[:, q0:q1, 0:HEAD], top[:, q0:q1, 0:HEAD], 0.5, None, ALU.max)

            def leave(q, into):
                return nc.vector.match_replace(into[0][:, q // GROUP, q % GROUP, :], entry_key[:, q, :],
                                               tile_keys[:, q, :], 0.0)

            def match_head(q):
                return nc.vector.tensor_tensor(match[q], tile_keys[:, q, :].unsqueeze(1).broadcast_to([P, HEAD, S]),
                                               entry_key[:, q, 0:HEAD].unsqueeze(2).broadcast_to([P, HEAD, S]),
                                               ALU.is_equal)

            def find_over_top(of, side):
                return nc.vector.max(of[2][:, side, 0:TOP], of[0][:, side, :, 0:REACH])

            def leave_over_top(of, side):
                return nc.vector.match_replace(of[1][:, side, :, 0:REACH], of[2][:, side, 0:TOP],
                                               of[0][:, side, :, 0:REACH], 0.0)

            def find_over_next(of, side):
                return nc.vector.max(of[2][:, side, TOP:ROUND], of[1][:, side, :, 0:REACH])

            def int_row(into, top_i):
                return nc.vector.tensor_scalar(into, top_i, STRIDE - 1, None, ALU.bitwise_and)

            def ahead_is_now(side):
                return nc.vector.tensor_copy(over_now[:, side, :], over_next[:, side, :])

            def share_slots(into, room):
                return nc.vector.tensor_tensor(into, next_row[:, 0, 0:ROUND],
                                               next_row[:, 1, bass.ds(room, ROUND)], ALU.bitwise_or)

            def load_room(pair):
                return dve.value_load(room_i[0:1, bass.ds(pair, 1)], min_val=0, max_val=ROUND)

            def make_lists(qs):
                for q in qs:
                    last = find_top(q)
                made(last)
                made(make_entry_keys(qs[0], qs[-1] + 1))
                for q in qs:
                    make_entry_row(q).then_inc(list_made, 1)

            def did(ins):
                ins.then_inc(pair_step, 1)
                steps[0] += 1
                return steps[0]

            def after(step):
                dve.wait_ge(pair_step, step)

            def place(q, j):
                m = S - j
                return nc.vector.copy_predicated(
                    dnn_in[:, q, 0:m, :], match[q][:, j, 0:m].unsqueeze(2).broadcast_to([P, m, E]),
                    packed[:, q, j, DNN].unsqueeze(1).broadcast_to([P, m, E]))

            def sum_head(t, q):
                return nc.vector.tensor_reduce(head_terms[:, bass.ds(t, 1), 0:E + 1],
                                               packed[:, q:q + 1, :, FM_LIN].rearrange("p q j e -> p q e j"),
                                               AX.X, ALU.add)

            def sum_squares(q):
                return nc.vector.tensor_tensor_reduce(out=square_sink[:], in0=packed[:, q, :, FM],
                                                      in1=packed[:, q, :, FM], scale=1.0, scalar=0.0,
                                                      op0=ALU.mult, op1=ALU.add,
                                                      accum_out=tile_squares[:, q:q + 1])

            def renew(pair, q, used):
                wait_alone(dve, tile_placed, SPAN * pair + q + 1)
                after(used)
                make_entry_row(q).then_inc(list_made, 1)
                nc.vector.tensor_copy(direct_row[:, q:q + 1, :], direct_rows[:, bass.ds(SPAN * (pair + 1) + q, 1), :]
                                      ).then_inc(direct_made, 1)
                did(match_head(q))

            def next_lists(pair):
                listed = [0]

                def step(ins):
                    ins.then_inc(list_step, 1)
                    listed[0] += 1

                def after_steps():
                    dve.wait_ge(list_step, listed[0])

                step(nc.vector.tensor_copy(ahead[0][:, 1, GROUP:GROUP + 1, 0:REACH],
                                           fillers[:, bass.ds(pair + 1, 1), :]))
                step(take_keys(pair + 1))
                after_steps()
                for q in range(SPAN):
                    step(find_top(q))
                after_steps()
                step(make_entry_keys(0, SPAN))
                after_steps()
                for q in range(SPAN):
                    step(leave(q, ahead))
                after_steps()
                for side in range(2):
                    step(find_over_top(ahead, side))
                after_steps()
                for side in range(2):
                    step(leave_over_top(ahead, side))
                after_steps()
                for side in range(2):
                    step(find_over_next(ahead, side))
                after_steps()
                step(nc.vector.tensor_copy(next_top_i[:], ahead[2][:, :, 0:ROUND]))
                after_steps()
                step(int_row(next_row[:, :, 0:ROUND], next_top_i[:]))
                after_steps()
                step(share_slots(next_over_row[:], load_room(pair + 1)))
                after_steps()
                dve.sem_clear(list_step)

            def tile_steps(pair, q):
                t = SPAN * pair + q
                used = steps[0]
                wait_alone(dve, head_landed[q], 16 * HEAD * (pair + 1))
                for j in range(HEAD):
                    if j == HEAD - 1:
                        place(q, j).then_inc(tile_placed, 1)
                    else:
                        placed = did(place(q, j))
                        if j == 0 and q:
                            renew(pair, q - 1, used)
                        after(placed)
                wait_alone(dve, direct_landed[q], 16 * DIRECT * (pair + 1))
                nc.vector.tensor_copy(dnn_in[:, q, S:F, :], packed[:, q, HEAD:HEAD + DIRECT, DNN]
                                      ).then_inc(direct_put, 1)
                squared = did(sum_squares(q))
                did(sum_head(t, q))
                if q == SPAN - 1:
                    after(squared)
                    did(nc.vector.tensor_copy(head_terms[:, bass.ds(SPAN * pair, SPAN), E + 1], tile_squares[:]))

            def take_tops(tops):
                nc.vector.tensor_copy(work_top_i[:], tops).then_inc(over_step, 1)
                nc.vector.tensor_scalar(work_key[:], tops, 0.5, None, ALU.max).then_inc(over_step, 1)
                dve.wait_ge(over_step, 2)
                nc.vector.tensor_scalar(work_tile[:], work_top_i[:], STRIDE_BITS, None, ALU.logical_shift_right
                                        ).then_inc(over_step, 1)
                dve.wait_ge(over_step, 3)
                nc.vector.tensor_tensor(work_of[:], work_tile[:].unsqueeze(1).broadcast_to([P, GROUP, ROUND]),
                                        tile_no[:].unsqueeze(2).broadcast_to([P, GROUP, ROUND]), ALU.is_equal
                                        ).then_inc(over_step, 1)
                return 4

            def take_rows(rows):
                return nc.vector.tensor_copy(work_rows[:, :, 0:ROW], rows)

            def match_over(side, j):
                return nc.vector.tensor_tensor(over_match[:, j % 3], now[0][:, side, 0:GROUP, 0:REACH],
                                               work_key[:, j:j + 1].unsqueeze(2).broadcast_to([P, GROUP, REACH]),
                                               ALU.is_equal)

            def place_over(side, j, step):
                q = side * GROUP
                nc.vector.copy_predicated(
                    dnn_in[:, q:q + GROUP, 0:REACH, :],
                    over_match[:, j % 3].unsqueeze(3).broadcast_to([P, GROUP, REACH, E]),
                    work_rows[:, j, DNN].unsqueeze(1).unsqueeze(1).broadcast_to([P, GROUP, REACH, E])
                ).then_inc(over_step, 1)
                if j + 2 >= ROUND:
                    return step + 1, step + 1
                match_over(side, j + 2).then_inc(over_step, 1)
                return step + 1, step + 2

            def sum_round(m, step, into):
                split = over_split[:, :, :, 0:m]
                nc.vector.tensor_tensor(over_squares[:, 0:m, :], work_rows[:, 0:m, FM], work_rows[:, 0:m, FM],
                                        ALU.mult).then_inc(over_step, 1)
                dve.wait_ge(over_step, step + 1)
                nc.vector.tensor_reduce(work_rows[:, 0:m, ROW], over_squares[:, 0:m, :], AX.X, ALU.add
                                        ).then_inc(over_step, 1)
                dve.wait_ge(over_step, step + 2)
                nc.vector.tensor_tensor(split, work_rows[:, 0:m, E:ROW + 1].rearrange("p j e -> p e j").unsqueeze(1)
                                        .broadcast_to([P, GROUP, TERMS, m]),
                                        work_of[:, :, 0:m].unsqueeze(2).broadcast_to([P, GROUP, TERMS, m]), ALU.mult
                                        ).then_inc(over_step, 1)
                dve.wait_ge(over_step, step + 3)
                return nc.vector.tensor_reduce(into, split, AX.X, ALU.add)

            def place_shared(mine, side, j, n, copied, step):
                if j == ROUND:
                    sum_round(j, step, mine).then_inc(over_placed, 1)
                    return
                with dve.If(n < ROUND - j if side else n > j):
                    dve.wait_ge(over_step, copied)
                    place_shared(mine, side, j + 1, n, *place_over(side, j, step))
                with dve.Else():
                    sum_round(j, step, mine).then_inc(over_placed, 1)

            def place_extra(mine, side, n, before):
                with dve.Fori(0, ROUNDS) as r:
                    with dve.If(n > r * ROUND):
                        dve.sem_clear(over_step)
                        step = take_tops(now[2][:, side, 0:ROUND])
                        nc.vector.tensor_copy(extra_top_i[:], work_top_i[:]).then_inc(over_step, 1)
                        dve.wait_ge(over_step, step + 1)
                        int_row(extra_row[:], extra_top_i[:]).then_inc(extra_list_made, 1)
                        match_over(side, 0).then_inc(over_step, 1)
                        match_over(side, 1).then_inc(over_step, 1)
                        wait_alone(dve, extra_landed, before + 16 * ROUND * (r + 1))
                        take_rows(over_packed[:, 0:ROUND, :]).then_inc(over_step, 1)
                        copied = step = step + 4
                        for j in range(ROUND):
                            dve.wait_ge(over_step, copied)
                            copied, step = place_over(side, j, step)
                        dve.wait_ge(over_step, step)
                        sum_round(ROUND, step, round_terms[:]).then_inc(over_step, 1)
                        dve.wait_ge(over_step, step + 4)
                        nc.vector.tensor_tensor(mine, mine, round_terms[:], ALU.add).then_inc(over_step, 1)
                        nc.vector.match_replace(now[0][:, side, :, 0:REACH], now[2][:, side, TOP:ROUND],
                                                now[1][:, side, :, 0:REACH], 0.0).then_inc(over_step, 1)
                        dve.wait_ge(over_step, step + 6)
                        find_over_top(now, side).then_inc(over_step, 1)
                        dve.wait_ge(over_step, step + 7)
                        leave_over_top(now, side).then_inc(over_step, 1)
                        dve.wait_ge(over_step, step + 8)
                        find_over_next(now, side).then_inc(over_step, 1)
                        dve.wait_ge(over_step, step + 9)

            def announce():
                after(steps[0])
                nc.vector.tensor_copy(over_row[:], next_over_row[:]).then_inc(over_list_made, 1)

            def load_front(pair):
                return (dve.value_load(slots_i[0:1, bass.ds(pair, 1)], min_val=0, max_val=ROUND),
                        dve.value_load(target_i[0:1, bass.ds(pair, 1)], min_val=1, max_val=16 * ROUND * PAIRS),
                        dve.value_load(shared_i[0:1, bass.ds(2 * pair, 1)], min_val=0, max_val=ROUND))

            def load_back(pair):
                group = 2 * pair + 1
                return (dve.value_load(start_i[0:1, bass.ds(pair, 1)], min_val=0, max_val=ROUND),
                        dve.value_load(shift_i[0:1, bass.ds(group, 1)], min_val=0, max_val=ROUND))

            def place_overflow(pair, side, loaded=None):
                group, first = 2 * pair + side, SPAN * pair + side * GROUP
                mine = all_over_terms[:, bass.ds(first, GROUP), :]
                wait_alone(dve, defaults_set, first + GROUP)
                after(steps[0])
                if side:
                    shared_slots, where, shift = loaded
                    rows, tops = over_packed[:, bass.ds(where, ROUND), :], now[2][:, 1, bass.ds(shift, ROUND)]
                else:
                    rows, tops = over_packed[:, 0:ROUND, :], now[2][:, 0, 0:ROUND]
                step = take_tops(tops)
                match_over(side, 0).then_inc(over_step, 1)
                match_over(side, 1).then_inc(over_step, 1)
                if side == 0:
                    shared_slots, target, where = load_front(pair)
                with dve.If(shared_slots > 0):
                    if side == 0:
                        wait_alone(dve, over_landed, target)
                    take_rows(rows).then_inc(over_step, 1)
                    dve.wait_ge(over_step, step + 3)
                    if side:
                        announce()
                    with dve.If(shift < ROUND if side else where > 0):
                        dve.wait_ge(over_step, step + 3)
                        place_shared(mine, side, 1, shift if side else where, *place_over(side, 0, step + 3))
                    with dve.Else():
                        nc.vector.memset(round_terms[:], 0.0).then_inc(over_placed, 1)
                with dve.Else():
                    dve.wait_ge(over_step, step + 2)
                    own = dve.value_load(extra_i[0:1, bass.ds(group, 1)], min_val=0, max_val=GROUP * REACH)
                    with dve.If(own > 0):
                        before = dve.value_load(before_i[0:1, bass.ds(group, 1)], min_val=0,
                                                max_val=16 * ROUND * ROUNDS * GROUPS)
                        place_extra(mine, side, own, before)
                    if side:
                        announce()
                    dve.sem_inc(over_placed, 1)
                loaded = None if side else (shared_slots, *load_back(pair))
                wait_alone(dve, over_placed, group + 1)
                dve.sem_clear(over_step)
                did(ahead_is_now(side))
                return loaded

            nc.vector.memset(last_terms[:], 0.0).then_inc(cleared, 1)
            nc.vector.memset(keys[:, TILES:TILES + SPAN, :], 0.0)
            nc.vector.memset(direct_rows[:, TILES:TILES + SPAN, :], 0)
            nc.vector.memset(room_i[:], 0)
            nc.vector.memset(slots_i[:], 0)
            nc.vector.memset(next_row[:], 0)
            nc.vector.memset(fillers[:], 0.0)
            nc.vector.memset(at_last[:], 0.0)
            nc.vector.memset(all_over_terms[:], 0.0)
            nc.vector.memset(over_packed[:], 0.0)
            made(nc.vector.memset(entry_key[:], -1.0))
            dve.wait_ge(base_made, GROUP + 3)
            nc.vector.tensor_scalar(filler[:], slot_no[:], float(STRIDE), float((GROUP + 1) * STRIDE),
                                    ALU.mult, ALU.add)
            dve.wait_ge(idx_loaded, 16)
            first, rest = slice(0, GROUP), slice(GROUP, TILES)
            made(cap(first))
            nc.vector.tensor_tensor(direct_based[:], capped[:, first, S:F], key_base[:, :, S:F], ALU.add
                                    ).then_inc(key_step, 1)
            steps[0] += 1
            made(make_wrap(first))
            nc.vector.tensor_tensor(direct_row[:, 0:GROUP], direct_based[:], wrap[:, first, S:F], ALU.add
                                    ).then_inc(direct_made, GROUP)
            made(make_values(first))
            made(make_based(first, 1))
            made(make_keys(first))
            made(nc.vector.tensor_copy(tile_keys[:, 0:GROUP, :], keys[:, first, :]))
            make_lists([0])
            made(cap(rest))
            made(make_wrap(rest))
            made(make_values(rest))
            nc.vector.tensor_scalar(at_last[:, :, 0:S], value[:, :, 0:S], float(V - 1), None, ALU.is_equal
                                    ).then_inc(at_last_made, 1)
            dve.wait_ge(at_last_made, 1)
            made(nc.vector.tensor_reduce(last_count[:], at_last[:], AX.X, ALU.add))
            made(nc.vector.tensor_scalar(beyond[:], last_count[:], -1.0, float(S - HEAD), ALU.mult, ALU.add))
            made(nc.vector.tensor_scalar(left[:], beyond[:], 0.0, None, ALU.max))
            nc.vector.tensor_reduce(over_length[:, 0:GROUPS], left[:].rearrange("p (g q) -> p g q", q=GROUP), AX.X,
                                    ALU.add).then_inc(lengths_made, 1)
            nc.vector.tensor_reduce(over_length[:, GROUPS:], left[:].rearrange("p (g q) -> p g q", q=SPAN), AX.X,
                                    ALU.add).then_inc(lengths_made, 1)
            make_lists(range(1, GROUP))
            made(make_based(rest, GROUPS - 1))
            nc.vector.tensor_copy(direct_row[:, GROUP:], based[:, GROUP:SPAN, S:F]).then_inc(direct_made, GROUP)
            made(make_keys(rest))
            made(nc.vector.tensor_copy(tile_keys[:, GROUP:, :], keys[:, GROUP:SPAN, :]))
            make_lists(range(GROUP, SPAN))
            dve.wait_ge(lengths_t, 1)
            nc.vector.tensor_reduce(longest[:], len_ps[0:GROUPS + PAIRS, :], AX.X, ALU.max).then_inc(longest_made, 1)
            dve.wait_ge(lengths_made, 2)
            made(nc.vector.tensor_scalar(free_slots[:], over_length[:, 0:GROUPS], -1.0, float(ROUND), ALU.mult, ALU.add))
            for pair in range(PAIRS):
                back = free_slots[:, 2 * pair + 1:2 * pair + 2]
                last = nc.vector.scalar_tensor_tensor(out=fillers[:, pair, :], in0=slot_no[:], scalar=back,
                                                      in1=filler[:], op0=ALU.is_lt, op1=ALU.mult)
            made(last)
            made(nc.vector.memset(over_now[:], 0.0))
            nc.vector.tensor_copy(now[0][:, 1, GROUP, 0:REACH], fillers[:, 0, :]).then_inc(key_step, 1)
            steps[0] += 1
            for q in range(SPAN):
                last = leave(q, now)
            made(last)
            for step in find_over_top, leave_over_top, find_over_next:
                for side in range(2):
                    last = step(now, side)
                made(last)
            made(nc.vector.tensor_copy(next_top_i[:], now[2][:, :, 0:ROUND]))
            made(int_row(next_row[:, :, 0:ROUND], next_top_i[:]))
            dve.wait_ge(longest_t, 1)
            made(nc.vector.tensor_copy(longest_row[:], len_ps[0:1, 0:GROUPS + PAIRS]))
            made(nc.vector.tensor_scalar(fits[:], longest_row[:, GROUPS:], float(ROUND), None, ALU.is_le))
            made(nc.vector.tensor_tensor(slots[:], longest_row[:, GROUPS:], fits[:], ALU.mult))
            nc.vector.tensor_copy(slots_i[:, 0:PAIRS], slots[:]).then_inc(key_step, 1)
            nc.vector.tensor_scalar(room_i[:, 0:PAIRS], slots[:], -1.0, float(ROUND), ALU.mult, ALU.add
                                    ).then_inc(key_step, 1)
            steps[0] += 2

            def by_pair(row):
                return row.rearrange("a (p s) -> a p s", s=2)

            made(nc.vector.tensor_tensor(by_pair(shared[:]), by_pair(longest_row[:, 0:GROUPS]),
                                         fits[:].unsqueeze(2).broadcast_to([1, PAIRS, 2]), ALU.mult))
            made(nc.vector.tensor_tensor(extra[:], longest_row[:, 0:GROUPS], shared[:], ALU.subtract))
            nc.vector.tensor_copy(extra_i[:], extra[:]).then_inc(over_known, 1)
            dve.wait_ge(over_known, 1)
            share_slots(over_row[:], load_room(0)).then_inc(over_list_made, 1)
            nc.vector.memset(zeros_row[:], 0.0)
            nc.vector.tensor_copy(shared_i[:], shared[:])
            nc.vector.tensor_scalar(shift_i[:], shared[:], -1.0, float(ROUND), ALU.mult, ALU.add)
            nc.vector.tensor_tensor(start_i[:], slots[:], by_pair(shared[:])[:, :, 1], ALU.subtract)
            made(nc.vector.tensor_scalar(extra_up[:], extra[:], float(ROUND - 1), None, ALU.add))
            made(nc.vector.tensor_scalar(rounds_i[:], extra_up[:], RIGHT_SHIFT, None, ALU.logical_shift_right))
            made(nc.vector.tensor_copy(rounds[:], rounds_i[:]))
            nc.vector.tensor_tensor_scan(slots_so_far[:], slots[:], zeros_row[:, 0:PAIRS], 0.0, ALU.add, ALU.add
                                         ).then_inc(key_step, 1)
            steps[0] += 1
            made(nc.vector.tensor_tensor_scan(rounds_so_far[:], rounds[:], zeros_row[:], 0.0, ALU.add, ALU.add))
            nc.vector.tensor_scalar(slots[:], slots_so_far[:], 16.0, 1.0, ALU.mult, ALU.max).then_inc(key_step, 1)
            steps[0] += 1
            made(nc.vector.tensor_tensor(rounds_before[:], rounds_so_far[:], rounds[:], ALU.subtract))
            nc.vector.tensor_copy(target_i[:], slots[:]).then_inc(key_step, 1)
            steps[0] += 1
            made(nc.vector.tensor_scalar(before_i[:], rounds_before[:], float(16 * ROUND), None, ALU.mult))
            made(nc.vector.memset(over_next[:], 0.0))
            for q in range(SPAN):
                last = match_head(q)
            made(last)
            nc.vector.tensor_copy(direct_rows[:, SPAN:TILES], based[:, SPAN:TILES, S:F]).then_inc(over_known, 1)
            dve.wait_ge(small_loaded, 16 * 8)
            nc.vector.tensor_scalar(const_c[:, 0:1], b3_c, wf1_c, bf_c, ALU.mult, ALU.add).then_inc(const_step, 1)
            dve.wait_ge(const_step, 1)
            nc.vector.tensor_scalar(const_c[:, 1:2], fm_bias_c, wf0_c, const_c[:, 0:1], ALU.mult, ALU.add
                                    ).then_inc(const_step, 1)
            dve.wait_ge(over_known, 2)

            with dve.Fori(0, PAIRS) as pair:
                steps[0] = 0
                with dve.If(pair < PAIRS - 1):
                    next_lists(pair)
                loaded = place_overflow(pair, 0)
                for q in range(SPAN):
                    if q == BACK_TILE:
                        place_overflow(pair, 1, loaded)
                    tile_steps(pair, q)
                renew(pair, SPAN - 1, steps[0])
                after(steps[0])
                dve.sem_clear(pair_step)

            def ended(n, ins):
                ins.then_inc(end_step, 1)
                dve.wait_ge(end_step, n)

            dve.wait_ge(share_kept, 1)
            ended(1, nc.vector.tensor_tensor(fetched_terms[:], all_over_terms[:], last_share[:], ALU.add))
            ended(2, nc.vector.tensor_tensor(terms[:], fetched_terms[:], head_terms[:], ALU.add))
            ended(3, nc.vector.tensor_tensor(fm_sum_sq[:], terms[:, :, 0:E], terms[:, :, 0:E], ALU.mult))
            ended(4, nc.vector.tensor_reduce(sq_of_sum[:], fm_sum_sq[:], AX.X, ALU.add))
            ended(5, nc.vector.tensor_tensor(pair_diff[:], sq_of_sum[:], terms[:, :, E + 1], ALU.subtract))
            ended(6, nc.vector.scalar_tensor_tensor(out=fm_out[:], in0=pair_diff[:], scalar=0.5, in1=terms[:, :, E],
                                                    op0=ALU.mult, op1=ALU.add))
            dve.wait_ge(const_step, 2)
            ended(7, nc.vector.tensor_scalar(fm_part[:], fm_out[:], wf0_c, const_c[:, 1:2], ALU.mult, ALU.add))
            dve.wait_ge(dnn_done, TILES)
            nc.vector.scalar_tensor_tensor(out=logit[:], in0=dnn_ps, scalar=wf1_c, in1=fm_part[:],
                                           op0=ALU.mult, op1=ALU.add).then_inc(logit_done, 1)

        @block.tensor
        def _(pe):
            pe.wait_ge(ident_made, 2)
            pe.wait_ge(lengths_made, 2)
            nc.tensor.transpose(len_ps[0:GROUPS + PAIRS, :], over_length[:], ident[:]).then_inc(lengths_t, 1)
            pe.wait_ge(longest_made, 1)
            nc.tensor.transpose(len_ps[0:1, 0:GROUPS + PAIRS], longest[:],
                                ident[0:GROUPS + PAIRS, 0:GROUPS + PAIRS]).then_inc(longest_t, 1)
            pe.wait_ge(at_last_made, 1)
            for g in range(GROUPS):
                last = nc.tensor.transpose(mask_ps[:, g, :],
                                           at_last[:, g * GROUP:(g + 1) * GROUP, :].rearrange("p t f -> p (t f)"),
                                           ident[:])
            last.then_inc(mask_t, 1)
            pe.wait_ge(over_known, 2)
            pe.wait_ge(last_terms_made, GROUP)
            pe.wait_ge(mask_t_kept, 1)
            for g in range(GROUPS):
                last = nc.tensor.matmul(share_ps[:, g * GROUP:(g + 1) * GROUP, :].rearrange("p t n -> p (t n)"),
                                        lhsT=at_last_t[:, g, :], rhs=last_terms[:].rearrange("p q n -> p (q n)"),
                                        start=True, stop=True)
            last.then_inc(share_made, 1)
            pe.wait_ge(share_kept, 1)
            pe.wait_ge(w1_loaded, 48)
            pe.wait_ge(small_loaded, 16 * 8)

            def second_layer(t):
                wait_alone(pe, h1_kept, t + 1)
                nc.tensor.matmul(h2_ps, lhsT=w2[:], rhs=h1[:], start=True, stop=True).then_inc(h2_done, 1)

            def output_layer(t):
                pe.wait_ge(h2_kept, t + 1)
                nc.tensor.matmul(dnn_ps[:, bass.ds(t, 1)], lhsT=h2[:], rhs=w3[:], start=True, stop=True
                                 ).then_inc(dnn_done, 1)

            with pe.Fori(0, PAIRS) as pair:
                for q in range(SPAN):
                    t, k = SPAN * pair + q, q % 2
                    pe.wait_ge(tile_placed, t + 1)
                    for c, (f, n) in enumerate(CHUNKS[:-1]):
                        last = nc.tensor.transpose(dnn_tp[k][0:n * E, c, :],
                                                   dnn_in[:, q, f:f + n, :].rearrange("p f e -> p (f e)"), ident[:])
                    last.then_inc(transposed, 1)
                    wait_alone(pe, direct_put, t + 1)
                    nc.tensor.transpose(direct_tp[0:DIRECT * E, :],
                                        dnn_in[:, q, S:F, :].rearrange("p f e -> p (f e)"), ident[:]
                                        ).then_inc(direct_transposed, 1)
                    if q:
                        second_layer(t - 1)
                    for c, (f, n) in enumerate(CHUNKS):
                        if c == 0:
                            wait_alone(pe, dnn_t_kept, 3 * t + 1)
                        elif c >= FULL:
                            wait_alone(pe, dnn_t_kept, 3 * t + 2 + c - FULL)
                        last = nc.tensor.matmul(h1_ps, lhsT=w1[0:n * E, c, :], rhs=dnn_t[k][0:n * E, c, :],
                                                start=c == 0, stop=c == len(CHUNKS) - 1)
                    last.then_inc(h1_done, 1)
                    if q:
                        output_layer(t - 1)
                    if q == SPAN - 1:
                        second_layer(t)
                        output_layer(t)

        @block.scalar
        def _(act):
            nc.scalar.preload_act_table(ACT.Sigmoid)
            act.dma_start(w2[:], W2).then_inc(small_loaded, 16)
            act.dma_start(w3[:], W3).then_inc(small_loaded, 16)
            act.dma_start(b1c[:], b1.unsqueeze(1)).then_inc(small_loaded, 16)
            act.dma_start(b2c[:], b2.unsqueeze(1)).then_inc(small_loaded, 16)
            act.dma_start(fm_bias_c, fm_bias.unsqueeze(0).broadcast_to([P, 1])).then_inc(small_loaded, 16)
            act.dma_start(b3_c, b3.unsqueeze(0).broadcast_to([P, 1])).then_inc(small_loaded, 16)
            act.dma_start(bf_c, bf.unsqueeze(0).broadcast_to([P, 1])).then_inc(small_loaded, 16)
            act.dma_start(scal[:, 3:5], Wf.rearrange("a b -> b a").broadcast_to([P, 2])).then_inc(small_loaded, 16)

            def set_defaults(q):
                nc.scalar.copy(dnn_in[:, q, 0:S, :], last_dnn[:]).then_inc(defaults_set, 1)

            act.wait_ge(last_loaded, 16 * (GROUP + 1))
            for q in range(SPAN):
                set_defaults(q)
            for q in range(GROUP):
                fields = slice(q * SLAB, q * SLAB + S)
                nc.scalar.activation(last_square_sink[fields, :], last_terms[fields, q, 0:E], ACT.Square,
                                     accum_out=last_terms[fields, q, E + 1:TERMS]).then_inc(last_terms_made, 1)
            act.wait_ge(mask_t, 1)
            nc.scalar.copy(at_last_t[:], mask_ps).then_inc(mask_t_kept, 1)
            act.wait_ge(share_made, 1)
            nc.scalar.copy(last_share[:], share_ps).then_inc(share_kept, 1)
            act.wait_ge(small_loaded, 16 * 8)

            def second_relu(t):
                act.wait_ge(h2_done, t + 1)
                nc.scalar.activation(h2[:], h2_ps, ACT.Relu, bias=b2c[:, 0:1]).then_inc(h2_kept, 1)

            with act.Fori(0, PAIRS) as pair:
                for q in range(SPAN):
                    t, k = SPAN * pair + q, q % 2
                    act.wait_ge(transposed, t + 1)
                    nc.scalar.copy(dnn_t[k][:, 0:FULL, :], dnn_tp[k][:, 0:FULL, :]).then_inc(dnn_t_kept, 1)
                    nc.scalar.copy(dnn_t[k][0:REST, FULL, :], dnn_tp[k][0:REST, FULL, :]).then_inc(dnn_t_kept, 1)
                    act.wait_ge(direct_transposed, t + 1)
                    nc.scalar.copy(dnn_t[k][0:DIRECT * E, FULL + 1, :], direct_tp[0:DIRECT * E, :]
                                   ).then_inc(dnn_t_kept, 1)
                    if q:
                        second_relu(t - 1)
                    act.wait_ge(h1_done, t + 1)
                    nc.scalar.activation(h1[:], h1_ps, ACT.Relu, bias=b1c[:, 0:1]).then_inc(h1_kept, 1)
                    set_defaults(q)
                    if q == SPAN - 1:
                        second_relu(t)

            act.wait_ge(logit_done, 1)
            nc.scalar.activation(y[:], logit[:], ACT.Sigmoid).then_inc(y_done, 1)


DIRECT_FIELDS = (1, 20, 21, 22)
_NAMES = ["r_idx", "rows", "fm_bias", "W1", "b1", "W2", "b2", "W3", "b3", "Wf", "bf"]


def kernel(**inputs):
    import numpy as np
    import concourse.bacc as bacc
    from concourse.bass_utils import run_bass_kernel_spmd

    given = {n: np.asarray(inputs[n if n == "r_idx" else "L0_rec_" + n]) for n in _NAMES if n != "rows"}
    dnn_emb, fm_emb, lin_w = (np.asarray(inputs["L0_rec_" + n]) for n in ("dnn_emb", "fm_emb", "lin_w"))
    F, V, E = dnn_emb.shape
    order = [f for f in range(F) if f not in DIRECT_FIELDS] + list(DIRECT_FIELDS)
    dnn_emb, fm_emb, lin_w = dnn_emb[order], fm_emb[order], lin_w[order]
    given["r_idx"] = given["r_idx"][:, order]
    given["W1"] = given["W1"].reshape(F, E, -1)[order].reshape(F * E, -1)
    rows = np.zeros((1 + F * V, 2 * E + 1), dnn_emb.dtype)
    rows[1:] = np.concatenate([dnn_emb, fm_emb, lin_w[:, :, None]], axis=2).reshape(F * V, 2 * E + 1)
    given["rows"] = rows
    given["fm_bias"] = given["fm_bias"].reshape(1)

    nc = bacc.Bacc("TRN2", target_bir_lowering=False, num_devices=1)
    arrays, args = {}, []
    for name in _NAMES:
        a = np.ascontiguousarray(given[name])
        arrays[f"in_{name}"] = a
        args.append(nc.dram_tensor(f"in_{name}", a.shape, mybir.dt.from_np(a.dtype), kind="ExternalInput").ap())
    B = given["r_idx"].shape[0]
    args.append(nc.dram_tensor("out", (B,), F32, kind="ExternalOutput").ap())
    deepfm_kernel(nc, *args, V, len(DIRECT_FIELDS))
    r = run_bass_kernel_spmd(nc, [arrays], core_ids=[0])
    return r.results[0]["out"]
```
